# Optimizing a Trainium2 kernel written in Bass

```python
import numpy as np
import jax
import jax.numpy as jnp

def _softmax(x, axis=-1):
    return jax.nn.softmax(x, axis=axis)

def _gelu(x):
    return jax.nn.gelu(x, approximate=True)

def _silu(x):
    return jax.nn.silu(x)

def _sigmoid(x):
    return jax.nn.sigmoid(x)

def _layernorm(x, axis=-1, eps=1e-05):
    m = jnp.mean(x, axis=axis, keepdims=True)
    v = jnp.var(x, axis=axis, keepdims=True)
    return (x - m) / jnp.sqrt(v + eps)

def _scatter_add(tgt, idx, src, axis=0):
    return tgt.at[idx].add(src)

def _segment_sum(src, seg, n):
    return jax.ops.segment_sum(src, seg, n)
kernel_name = 'mk_prb_d1_jaxref_r8_ec6bf3'

def setup_inputs(seed: int=0):
    np.random.seed(seed)
    _w = jnp.asarray

    def _L0_attn_setup():
        import jax, jax.numpy as jnp
        import numpy as np
        import math
        EMB = 128
        HEADS = 16
        B, S = (2, 256)
        key = jax.random.key(seed)
        k_x, k_wq, k_bq, k_wu, k_bu = jax.random.split(key, 5)
        lim = 1.0 / math.sqrt(EMB)
        x = jax.random.normal(k_x, (B, S, EMB), dtype=jnp.float32)
        wq = jax.random.uniform(k_wq, (EMB, EMB), jnp.float32, -lim, lim)
        bq = jax.random.uniform(k_bq, (EMB,), jnp.float32, -lim, lim)
        wu = jax.random.uniform(k_wu, (EMB, EMB), jnp.float32, -lim, lim)
        bu = jax.random.uniform(k_bu, (EMB,), jnp.float32, -lim, lim)
        return {'x': x, 'wq': wq, 'bq': bq, 'wu': wu, 'bu': bu}
    _L0_attn_in = _L0_attn_setup()

    def _L0_ffn_setup():
        import jax, jax.numpy as jnp
        import numpy as np
        D_IN, D_HID = (128, 512)

        def _ternary(key, shape):
            return jax.random.randint(key, shape, -1, 2).astype(jnp.float32)

        def _tlin(x, w, s):
            return jnp.einsum('bsi,oi->bso', x, w) * s
        key = jax.random.key(seed)
        ks = jax.random.split(key, 12)
        inv = lambda fan: 1.0 / np.sqrt(fan).astype(np.float32)
        return {'x': jax.random.normal(ks[0], (4, 256, D_IN), dtype=jnp.float32), 'w1_w': _ternary(ks[1], (D_HID, D_IN)), 'w1_s': jax.random.uniform(ks[2], (D_HID,), dtype=jnp.float32) * inv(D_IN), 'w2_w': _ternary(ks[3], (D_HID, D_IN)), 'w2_s': jax.random.uniform(ks[4], (D_HID,), dtype=jnp.float32) * inv(D_IN), 'h1_w': _ternary(ks[5], (D_HID, D_HID)), 'h1_s': jax.random.uniform(ks[6], (D_HID,), dtype=jnp.float32) * inv(D_HID), 'h2_w': _ternary(ks[7], (D_HID, D_HID)), 'h2_s': jax.random.uniform(ks[8], (D_HID,), dtype=jnp.float32) * inv(D_HID), 'w3_w': _ternary(ks[9], (D_IN, D_HID)), 'w3_s': jax.random.uniform(ks[10], (D_IN,), dtype=jnp.float32) * inv(D_HID)}
    _L0_ffn_in = _L0_ffn_setup()
    _d = {'L0_attn_x': _L0_attn_in['x'], 'L0_attn_wq': _L0_attn_in['wq'], 'L0_attn_bq': _L0_attn_in['bq'], 'L0_attn_wu': _L0_attn_in['wu'], 'L0_attn_bu': _L0_attn_in['bu'], 'L0_ffn_w1_w': _L0_ffn_in['w1_w'], 'L0_ffn_w1_s': _L0_ffn_in['w1_s'], 'L0_ffn_w2_w': _L0_ffn_in['w2_w'], 'L0_ffn_w2_s': _L0_ffn_in['w2_s'], 'L0_ffn_h1_w': _L0_ffn_in['h1_w'], 'L0_ffn_h1_s': _L0_ffn_in['h1_s'], 'L0_ffn_h2_w': _L0_ffn_in['h2_w'], 'L0_ffn_h2_s': _L0_ffn_in['h2_s'], 'L0_ffn_w3_w': _L0_ffn_in['w3_w'], 'L0_ffn_w3_s': _L0_ffn_in['w3_s']}
    _x0 = _d['L0_attn_x']
    _d['L0_attn_x'] = jax.random.normal(jax.random.fold_in(jax.random.key(seed), 1), (32, 256, 128), dtype=_x0.dtype)
    del _x0
    return _d

def reference(L0_attn_x, L0_attn_wq, L0_attn_bq, L0_attn_wu, L0_attn_bu, L0_ffn_w1_w, L0_ffn_w1_s, L0_ffn_w2_w, L0_ffn_w2_s, L0_ffn_h1_w, L0_ffn_h1_s, L0_ffn_h2_w, L0_ffn_h2_s, L0_ffn_w3_w, L0_ffn_w3_s):

    def _L0_attn_ref(x, wq, bq, wu, bu):
        import jax, jax.numpy as jnp
        import numpy as np
        import math
        EMB = 128
        HEADS = 16
        B, S = (2, 256)
        b, s, emb = x.shape
        hd = emb // HEADS
        q = jnp.einsum('bse,oe->bso', x, wq) + bq
        qh = q.reshape(HEADS, b, s, hd)
        kh = qh
        vh = qh
        scale = 1.0 / math.sqrt(emb)
        scores = jnp.einsum('hbqd,hbkd->hbqk', qh, kh) * scale
        attn = jax.nn.softmax(scores, axis=-1)
        out = jnp.einsum('hbqk,hbkd->hbqd', attn, vh)
        out = out.reshape(b, s, emb)
        return jnp.einsum('bse,oe->bso', out, wu) + bu

    def _L0_ffn_ref(x, w1_w, w1_s, w2_w, w2_s, h1_w, h1_s, h2_w, h2_s, w3_w, w3_s):
        import jax, jax.numpy as jnp
        import numpy as np
        D_IN, D_HID = (128, 512)

        def _ternary(key, shape):
            return jax.random.randint(key, shape, -1, 2).astype(jnp.float32)

        def _tlin(x, w, s):
            return jnp.einsum('bsi,oi->bso', x, w) * s
        h = jax.nn.silu(_tlin(x, w1_w, w1_s)) * _tlin(x, w2_w, w2_s)
        h = jax.nn.gelu(_tlin(h, h1_w, h1_s), approximate=False)
        h = jax.nn.gelu(_tlin(h, h2_w, h2_s), approximate=False)
        return _tlin(h, w3_w, w3_s)
    x = L0_attn_x
    xn = _layernorm(x, axis=-1)
    x = x + _L0_attn_ref(xn, L0_attn_wq, L0_attn_bq, L0_attn_wu, L0_attn_bu) + _L0_ffn_ref(xn, L0_ffn_w1_w, L0_ffn_w1_s, L0_ffn_w2_w, L0_ffn_w2_s, L0_ffn_h1_w, L0_ffn_h1_s, L0_ffn_h2_w, L0_ffn_h2_s, L0_ffn_w3_w, L0_ffn_w3_s)
    return x

_drawn_inputs = setup_inputs


def setup_inputs(seed=0):
    import zlib

    import numpy as np

    out = dict(_drawn_inputs(seed))
    spreads = {}
    factors = {}
    for name, (base, spread) in spreads.items():
        noise = np.random.default_rng([zlib.crc32(name.encode()), seed]).standard_normal(out[name].shape)
        drawn = base * np.exp(spread * noise) if base else spread * noise
        out[name] = jnp.asarray(drawn.astype(out[name].dtype))
    for name, factor in factors.items():
        out[name] = (out[name] * factor).astype(out[name].dtype)
    return out
```

```python
from contextlib import ExitStack

import numpy as np
import concourse.bass as bass
from concourse import mybir
from concourse.alu_op_type import AluOpType as ALU

F32 = mybir.dt.float32
F32R = mybir.dt.float32r
BF16 = mybir.dt.bfloat16
I32 = mybir.dt.int32
ACT = mybir.ActivationFunctionType
AX = mybir.AxisListType

BATCH, SEQ, EMB, HID = 32, 256, 128, 512
TOKENS = BATCH * SEQ
P = 128
HEADS = 16
HD = EMB // HEADS
NJ = EMB // HD
HEAD_TOK = SEQ // NJ
POS = SEQ
EPS = 1e-5
SCORE_SCALE = 1.0 / float(np.sqrt(EMB))

TT = 512
SUB = TT // P
KB = HID // P
PAIRS = TOKENS // (2 * TT)
HF_RING = 4
OPS = 3 * 2 * KB
FF_SLOTS = 3

W1, W2, H1, H2 = 0, HID, 2 * HID, (2 + KB) * HID
W3 = H2 + KB * HID
WQ = W3 + KB * P
WCOLS = WQ + P

AT = 256
NB = AT // HEAD_TOK
A_TILES = TOKENS // AT
COLG = 4
GROUPS = NB // COLG
NBUF = 4
CHUNKS = POS // P
ROWS = 6 * HD
PARTS_OF_KEYS, PARTS_OF_QUERIES = (0, 0, 0, 1, 1, 2), (0, 1, 2, 0, 1, 0)
PV_ROWS = 32
LOADS = ((0, 0, 1), (1, 0, 1), (2, 0, 2), (4, 1, 2)), ((0, 0, 3), (3, 0, 2), (5, 0, 1))
KEYS_LOADED, QUERIES_LOADED = 16 * len(LOADS[0]), 16 * len(LOADS[1])


def block_of(k):
    return COLG * (k % COLG) + k // COLG


def wait_alone(engine, semaphore, value, passed):
    engine.wait_ge(semaphore, value)
    engine.sem_inc(passed, 1)


def feed_forward(nc, io, mem, sem):
    ps_ff, ps_prep = mem["ps_ff"], mem["ps_prep"]
    w_hi, w_lo, h_hi, h_lo = mem["w_hi"], mem["w_lo"], mem["h_hi"], mem["h_lo"]
    hf, silu_out, y_sum = mem["hf"], mem["silu_out"], mem["y_sum"]
    x_nat, xn_nat, xn_hi, xn_lo = mem["x_nat"], mem["xn_nat"], mem["xn_hi"], mem["xn_lo"]
    q_full, q_rest, q_part = mem["q_full"], mem["q_rest"], mem["q_part"]
    stats, moments, var_eps, rstd = mem["stats"], mem["moments"], mem["var_eps"], mem["rstd"]
    scales, bias_q = mem["scales"], mem["bias_q"]
    FREE = 2

    def slot_is_free(pe, p, j):
        before, pair = (j - FF_SLOTS, p) if j >= FF_SLOTS else (j - FF_SLOTS + 18, p - 1)
        if before < 8:
            pe.wait_ge(sem["gated"], FREE + 8 * pair + before + 1)
        elif before < 16:
            pe.wait_ge(sem["gelu_full"], 16 + 16 * pair + 2 * (before - 8) + 2)
        else:
            pe.wait_ge(sem["ff_added"], FREE + 2 * pair + before - 16 + 1)

    def h_ready(pe, p, k):
        pe.wait_ge(sem["h_hi_done"], HF_RING + OPS * p + k)
        pe.wait_ge(sem["h_lo_done"], HF_RING + OPS * p + k)

    with nc.Block() as block:
        @block.sync
        def _(sp):
            def load_x(u, pair, first):
                if not first:
                    wait_alone(sp, sem["sub_normed"], 2 * SUB * pair, sem["sp_passed"])
                src = io["x"].rearrange("(n s p) e -> p n s e", p=P, s=SUB)
                if first:
                    src = src[:, u]
                else:
                    src = src[:, bass.ds(2 * pair + u, 1)].rearrange("p o s e -> p (o s) e")
                sp.dma_start(x_nat[:, u], src).then_inc(sem[f"x_loaded{u}"], 16)

            for u in range(2):
                load_x(u, 0, True)
            staged = y_sum[:, TOKENS - WCOLS:]
            for n, (name, at, blocks, cols) in enumerate((("w1", W1, 1, HID), ("w2", W2, 1, HID), ("h1", H1, KB, HID),
                                                          ("h2", H2, KB, HID), ("w3", W3, KB, P), ("wq", WQ, 1, P))):
                to = staged[:, at:at + blocks * cols].rearrange("p (b c) -> p b c", c=cols)
                sp.dma_start(to, io[name].rearrange("(b p) c -> p b c", p=P)).then_inc(sem["w_loaded"], 16)
            wait_alone(sp, sem["w_split"], 2, sem["sp_passed"])
            half = TOKENS // 2
            sp.dma_start(y_sum[:, half:], io["xT"][:, half:]).then_inc(sem["xT_loaded"], 16)

            def store_q(u, pair):
                wait_alone(sp, sem["q_third"], 2 * pair + u + 1, sem["sp_passed"])
                to = io["q_parts"][:, :, bass.ds((2 * pair + u) * TT, TT)].rearrange("c f t -> f c t")
                sp.dma_start(to, q_part[:, u]).then_inc(sem[f"q_stored{u}"], 16)

            for u in range(2):
                store_q(u, 0)
            with sp.Fori(0, PAIRS - 1) as p:
                for u in range(2):
                    load_x(u, p + 1, False)
                for u in range(2):
                    store_q(u, p + 1)
            for u in range(2):
                wait_alone(sp, sem[f"q_stored{u}"], 16 + 16 * PAIRS, sem["sp_passed"])

        @block.gpsimd
        def _(pool):
            pool.dma_start(mem["ident"][:], io["ident"]).then_inc(sem["small_loaded"], 16)
            for n, name in enumerate(("w1s", "w2s", "h1s", "h2s")):
                pool.dma_start(scales[:, n * KB:(n + 1) * KB], io[name]).then_inc(sem["small_loaded"], 16)
            pool.dma_start(scales[:, 4 * KB:4 * KB + 1], io["w3s"]).then_inc(sem["small_loaded"], 16)
            pool.dma_start(bias_q[:], io["bq"]).then_inc(sem["small_loaded"], 16)
            pool.dma_start(y_sum[:, :TOKENS // 4], io["xT"][:, :TOKENS // 4]).then_inc(sem["xT_first"], 16)
            wait_alone(pool, sem["w_split"], 2, sem["pool_passed"])
            pool.dma_start(y_sum[:, TOKENS // 4:TOKENS // 2], io["xT"][:, TOKENS // 4:TOKENS // 2]).then_inc(sem["xT_second"], 16)
            pool.memset(mem["minus_half"][:], -0.5).then_inc(sem["const_set"], 1)
            wait_alone(pool, sem["const_set"], 1, sem["pool_passed"])

            def inverse_deviation(pair):
                wait_alone(pool, sem["var_ready"], pair + 1, sem["pool_passed"])
                nc.gpsimd.tensor_tensor(rstd[:], var_eps[:], mem["minus_half"][:], ALU.pow).then_inc(sem["rstd_ready"], 1)

            def q_remainders(pair):
                for u in range(2):
                    wait_alone(pool, sem["q_first"], 2 * pair + u + 1, sem["pool_passed"])
                    nc.gpsimd.tensor_tensor(q_rest[:, u], q_full[:, u], q_part[:, u, 0], ALU.subtract).then_inc(sem["q_rest_ready"], 1)
                for u in range(2):
                    wait_alone(pool, sem["q_second"], 2 * pair + u + 1, sem["pool_passed"])
                    nc.gpsimd.tensor_tensor(q_part[:, u, 2], q_rest[:, u], q_part[:, u, 1], ALU.subtract).then_inc(sem["q_third"], 1)

            inverse_deviation(0)
            q_remainders(0)
            with pool.Fori(0, PAIRS - 1) as p:
                inverse_deviation(p + 1)
                q_remainders(p + 1)

        @block.vector
        def _(dve):
            staged = y_sum[:, TOKENS - WCOLS:]
            dve.sem_inc(sem["gated"], FREE)
            dve.sem_inc(sem["ff_added"], FREE)
            dve.sem_inc(sem["h_lo_done"], HF_RING)
            dve.memset(mem["ones"][:], 1.0).then_inc(sem["const_set"], 2)
            dve.wait_ge(sem["w_loaded"], 6 * 16)
            dve.wait_ge(sem["w_hi_done"], 1)
            nc.vector.tensor_tensor(w_lo[:], staged, w_hi[:].bitcast(F32), ALU.subtract).then_inc(sem["w_split"], 2)
            dve.wait_ge(sem["w_split"], 2)
            nc.vector.tensor_reduce(out=mem["lo_max"][:], in_=w_lo[:, :WQ].bitcast(F32), axis=AX.X, op=ALU.max,
                                    apply_absolute_value=True).then_inc(sem["lo_max_ready"], 1)
            dve.wait_ge(sem["lo_sum_ready"], 1)
            nc.vector.tensor_scalar(mem["flag"][:], ps_prep[0:1, 0, 0:1], 0.0, None, ALU.not_equal).then_inc(sem["flag_ready"], 1)

            def norm_inputs(pair):
                for u in range(2):
                    dve.wait_ge(sem[f"x_loaded{u}"], 16 * (pair + 1))
                    for s in range(SUB):
                        nc.vector.bn_stats(out=stats[:, u * SUB + s], in_=x_nat[:, u, s]).then_inc(sem["stats_done"], 1)
                for n in range(2 * SUB):
                    if n == 0:
                        wait_alone(dve, sem["stats_done"], 2 * SUB * (pair + 1), sem["dve_passed"])
                    nc.vector.bn_aggr(out=moments[:, n], in_=stats[:, n]).then_inc(sem["moments_done"], 1)
                dve.wait_ge(sem["moments_done"], 2 * SUB * (pair + 1))
                nc.vector.tensor_scalar(var_eps[:], moments[:, :, 1], EPS, None, ALU.add).then_inc(sem["var_ready"], 1)
                dve.wait_ge(sem["rstd_ready"], pair + 1)
                dve.wait_ge(sem["transposed"], 2 + 2 * pair)
                for n in range(2 * SUB):
                    u, s = n // SUB, n % SUB
                    nc.vector.tensor_scalar(xn_nat[:, u, s], x_nat[:, u, s], moments[:, n, 0:1], rstd[:, n:n + 1],
                                            ALU.subtract, ALU.mult).then_inc(sem["sub_normed"], 1)

            def lo_part(p, k, layer, u, b):
                if layer == 0:
                    dve.wait_ge(sem["gated"], FREE + 8 * p + k + 1)
                else:
                    dve.wait_ge(sem["gelu_full"], 16 + 16 * p + (k - 8) + 1)
                dve.wait_ge(sem["h_hi_done"], HF_RING + OPS * p + k + 1)
                nc.vector.tensor_tensor(h_lo[:, layer % 2, u, b], hf[:, k % HF_RING], h_hi[:, layer % 2, u, b].bitcast(F32),
                                        ALU.subtract).then_inc(sem["h_lo_done"], 1)

            def xn_low(pair):
                for u in range(2):
                    dve.wait_ge(sem["xn_hi_done"], 2 * pair + u + 1)
                    nc.vector.tensor_tensor(xn_lo[:, u], ps_prep[:, u], xn_hi[:, u].bitcast(F32), ALU.subtract).then_inc(sem["xn_lo_done"], 1)

            def pair_of_tiles(p, more):
                for u in range(2):
                    for b in range(KB):
                        k, slot = KB * u + b, (KB * u + b) % FF_SLOTS
                        dve.wait_ge(sem["silu_done"], FREE + 8 * p + k + 1)
                        dve.wait_ge(sem["h_hi_done"], OPS * p + k + 1)
                        dve.wait_ge(sem["h_lo_done"], OPS * p + k + 1)
                        nc.vector.scalar_tensor_tensor(out=hf[:, k % HF_RING], in0=ps_ff[:, slot, 1], scalar=scales[:, KB + b:KB + b + 1],
                                                       in1=silu_out[:, k % 2], op0=ALU.mult, op1=ALU.mult).then_inc(sem["gated"], 1)
                        lo_part(p, k, 0, u, b)
                if more:
                    norm_inputs(p + 1)
                for u in range(2):
                    for b in range(KB):
                        lo_part(p, 8 + KB * u + b, 1, u, b)
                if more:
                    xn_low(p + 1)
                for u in range(2):
                    for b in range(KB):
                        lo_part(p, 16 + KB * u + b, 2, u, b)
                if more:
                    q_seconds(p + 1)
                for u in range(2):
                    slot = (16 + u) % FF_SLOTS
                    dve.wait_ge(sem["down_done"], 2 * p + u + 1)
                    to = y_sum[:, bass.ds((2 * p + u) * TT, TT)]
                    nc.vector.scalar_tensor_tensor(out=to, in0=ps_ff[:, slot, 0], scalar=scales[:, 4 * KB:4 * KB + 1], in1=to,
                                                   op0=ALU.mult, op1=ALU.add).then_inc(sem["ff_added"], 1)

            def q_seconds(pair):
                for u in range(2):
                    dve.wait_ge(sem["q_rest_ready"], 2 * pair + u + 1)
                    nc.vector.tensor_copy(q_part[:, u, 1], q_rest[:, u]).then_inc(sem["q_second"], 1)

            norm_inputs(0)
            xn_low(0)
            q_seconds(0)
            dve.wait_ge(sem["small_loaded"], 7 * 16)
            dve.wait_ge(sem["xT_first"], 16)
            dve.wait_ge(sem["xT_second"], 16)
            dve.wait_ge(sem["xT_loaded"], 16)
            with dve.Fori(0, PAIRS - 1) as p:
                pair_of_tiles(p, True)
            pair_of_tiles(PAIRS - 1, False)

        @block.scalar
        def _(act):
            act.sem_inc(sem["gelu_full"], 16)
            act.sem_inc(sem["h_hi_done"], HF_RING)
            act.sem_inc(sem["silu_done"], FREE)
            for u in range(2):
                act.sem_inc(sem[f"q_stored{u}"], 16)
            act.wait_ge(sem["w_loaded"], 6 * 16)
            nc.scalar.activation(w_hi[:], y_sum[:, TOKENS - WCOLS:], ACT.Identity).then_inc(sem["w_hi_done"], 1)
            act.wait_ge(sem["small_loaded"], 7 * 16)

            def xn_high(pair):
                for u in range(2):
                    act.wait_ge(sem["transposed"], 2 + 2 * pair + u + 1)
                    nc.scalar.activation(xn_hi[:, u], ps_prep[:, u], ACT.Identity).then_inc(sem["xn_hi_done"], 1)

            def q_out(pair):
                for u in range(2):
                    act.wait_ge(sem["q_product"], 2 * pair + u + 1)
                    act.wait_ge(sem[f"q_stored{u}"], 16 + 16 * pair)
                    nc.scalar.activation(q_full[:, u], ps_prep[:, u], ACT.Identity, bias=bias_q[:, 0:1])
                    nc.scalar.activation(q_part[:, u, 0], ps_prep[:, u], ACT.Identity, bias=bias_q[:, 0:1]).then_inc(sem["q_first"], 1)

            def silu(p, k):
                act.wait_ge(sem["up_done"], 8 * p + k + 1)
                act.wait_ge(sem["gated"], 8 * p + k + 1)
                nc.scalar.activation(silu_out[:, k % 2], ps_ff[:, k % FF_SLOTS, 0], ACT.Silu, scale=scales[:, k % KB:k % KB + 1]).then_inc(sem["silu_done"], 1)

            def high_copy(p, k):
                act.wait_ge(sem["gated"], FREE + 8 * p + k + 1)
                nc.scalar.activation(h_hi[:, 0, k // KB, k % KB], hf[:, k % HF_RING], ACT.Identity).then_inc(sem["h_hi_done"], 1)

            def gelu(p, layer, u, b):
                k = 8 * layer + KB * u + b
                slot = 8 + (k - 8) // 2
                src = ps_ff[:, slot % FF_SLOTS, b % 2]
                s = scales[:, (1 + layer) * KB + b:(1 + layer) * KB + b + 1]
                act.wait_ge(sem["hidden_done"], 16 * p + (k - 8) + 1)
                nc.scalar.activation(h_hi[:, layer % 2, u, b], src, ACT.Gelu, scale=s).then_inc(sem["h_hi_done"], 1)
                act.wait_ge(sem["h_lo_done"], OPS * p + k + 1)
                act.wait_ge(sem["h_hi_done"], OPS * p + k + 1)
                nc.scalar.activation(hf[:, k % HF_RING], src, ACT.Gelu, scale=s).then_inc(sem["gelu_full"], 1)

            def pair_of_tiles(p, more):
                silu(p, 0)
                for k in range(1, 2 * KB):
                    silu(p, k)
                    high_copy(p, k - 1)
                high_copy(p, 2 * KB - 1)
                for u in range(2):
                    for b in range(KB):
                        gelu(p, 1, u, b)
                if more:
                    xn_high(p + 1)
                for u in range(2):
                    for b in range(KB):
                        gelu(p, 2, u, b)
                    if more and u == 0:
                        q_out(p + 1)

            xn_high(0)
            q_out(0)
            with act.Fori(0, PAIRS - 1) as p:
                pair_of_tiles(p, True)
            pair_of_tiles(PAIRS - 1, False)

        @block.tensor
        def _(pe):
            pe.sem_inc(sem["transposed"], 2)
            pe.wait_ge(sem["lo_max_ready"], 1)
            pe.wait_ge(sem["const_set"], 3)
            nc.tensor.matmul(ps_prep[0:1, 0, 0:1], mem["lo_max"][:], mem["ones"][:], start=True, stop=True).then_inc(sem["lo_sum_ready"], 1)
            pe.wait_ge(sem["small_loaded"], 7 * 16)

            def transposes(pair, first):
                for u in range(2):
                    pe.wait_ge(sem["sub_normed"], 2 * SUB * pair + SUB * (u + 1))
                    if first:
                        pe.wait_ge(sem["flag_ready"], 1)
                    else:
                        pe.wait_ge(sem["q_first"], 2 * pair + u - 1)
                    for s in range(SUB):
                        last = nc.tensor.transpose(ps_prep[:, u, s * P:(s + 1) * P], xn_nat[:, u, s], mem["ident"][:])
                    last.then_inc(sem["transposed"], 1)

            def q_product(pair):
                for u in range(2):
                    pe.wait_ge(sem["xn_hi_done"], 2 * pair + u + 1)
                    pe.wait_ge(sem["xn_lo_done"], 2 * pair + u + 1)
                    terms = [(w, a) for w in (w_hi, w_lo) for a in (xn_hi, xn_lo)]
                    for n, (w, a) in enumerate(terms):
                        last = nc.tensor.matmul(ps_prep[:, u], w[:, WQ:WQ + P], a[:, u], start=(n == 0), stop=(n == len(terms) - 1))
                    last.then_inc(sem["q_product"], 1)

            def up(p, u, parts):
                for b in range(KB):
                    j = KB * u + b
                    slot_is_free(pe, p, j)
                    for half, at in ((0, W1), (1, W2)):
                        terms = [(w, a) for w in parts for a in (xn_hi, xn_lo)]
                        for n, (w, a) in enumerate(terms):
                            last = nc.tensor.matmul(ps_ff[:, j % FF_SLOTS, half], w[:, at + b * P:at + (b + 1) * P], a[:, u],
                                                    start=(n == 0), stop=(n == len(terms) - 1))
                    last.then_inc(sem["up_done"], 1)

            def hidden(p, layer, u, parts):
                at = (None, H1, H2)[layer]
                h_ready(pe, p, 8 * (layer - 1) + KB * (u + 1))
                for b in range(KB):
                    j = 8 + 4 * (layer - 1) + 2 * u + b // 2
                    if b % 2 == 0:
                        slot_is_free(pe, p, j)
                    terms = [(w, h, i) for i in range(KB) for w in parts for h in (h_hi, h_lo)]
                    for n, (w, h, i) in enumerate(terms):
                        c = at + i * HID + b * P
                        last = nc.tensor.matmul(ps_ff[:, j % FF_SLOTS, b % 2], w[:, c:c + P], h[:, (layer - 1) % 2, u, i],
                                                start=(n == 0), stop=(n == len(terms) - 1))
                    last.then_inc(sem["hidden_done"], 1)

            def down(p, u, parts):
                j = 16 + u
                slot_is_free(pe, p, j)
                h_ready(pe, p, 16 + KB * (u + 1))
                terms = [(w, h, i) for i in range(KB) for w in parts for h in (h_hi, h_lo)]
                for n, (w, h, i) in enumerate(terms):
                    c = W3 + i * P
                    last = nc.tensor.matmul(ps_ff[:, j % FF_SLOTS, 0], w[:, c:c + P], h[:, 0, u, i],
                                            start=(n == 0), stop=(n == len(terms) - 1))
                last.then_inc(sem["down_done"], 1)

            def pair_of_tiles(p, more, parts):
                up(p, 0, parts)
                up(p, 1, parts)
                hidden(p, 1, 0, parts)
                hidden(p, 1, 1, parts)
                if more:
                    transposes(p + 1, False)
                hidden(p, 2, 0, parts)
                if more:
                    q_product(p + 1)
                hidden(p, 2, 1, parts)
                down(p, 0, parts)
                down(p, 1, parts)

            def all_pairs(parts):
                with pe.Fori(0, PAIRS - 1) as p:
                    pair_of_tiles(p, True, parts)
                pair_of_tiles(PAIRS - 1, False, parts)

            transposes(0, True)
            q_product(0)
            general = pe.value_load(mem["flag"][0:1, 0:1])
            with pe.If(general != 0):
                all_pairs((w_hi, w_lo))
            with pe.Else():
                all_pairs((w_hi,))


FF_SEMS = ("sp_passed pool_passed dve_passed w_loaded w_hi_done w_split lo_max_ready lo_sum_ready flag_ready const_set small_loaded xT_first xT_second "
           "xT_loaded x_loaded0 x_loaded1 stats_done moments_done var_ready rstd_ready sub_normed transposed "
           "xn_hi_done xn_lo_done q_product q_first q_rest_ready q_second q_third q_stored0 q_stored1 up_done silu_done "
           "gated hidden_done gelu_full h_hi_done h_lo_done down_done ff_added").split()



MAX_FREE = EXP_FREE = PV_FREE = PROJ_FREE = Y_FREE = 2
SHIFT_DMAS = 16 * 3 * CHUNKS
STAGE_DMAS = 16 * COLG


class Tile:

    def __init__(self, lap, at):
        self.lap, self.at = lap, at

    def __add__(self, n):
        return Tile(self.lap, self.at + n)

    def number(self):
        return self.lap * NBUF + self.at

    def laps(self, ring):
        return self.lap * (NBUF // ring) + self.at // ring

    def exists(self):
        return not isinstance(self.lap, int) or 0 <= self.number() < A_TILES

    def past(self, n):
        return not isinstance(self.lap, int) or self.number() >= n


def steps(engine, step):
    loops = (A_TILES - 5) // NBUF
    for t in range(-2, 2):
        step(Tile(0, t))
    with engine.Fori(0, loops) as lap:
        for at in range(2, 2 + NBUF):
            step(Tile(lap, at))
    for t in range(2 + NBUF * loops, A_TILES + 2):
        step(Tile(0, t))


def attention(nc, io, mem, sem):
    qk, qq, v_aug, probs = mem["qk"], mem["qq"], mem["v_aug"], mem["probs"]
    ps_max, ps_exp, ps_pv, ps_misc = mem["ps_max"], mem["ps_exp"], mem["ps_pv"], mem["ps_misc"]
    row_max, neg_max, shift_rest, shift_part = mem["row_max"], mem["neg_max"], mem["shift_rest"], mem["shift_part"]
    o_stage, o_feat, y_sum = mem["o_stage"], mem["o_feat"], mem["y_sum"]
    JC = NJ // CHUNKS

    with nc.Block() as block:
        @block.sync
        def _(sp):
            sp.dma_start(mem["pick"][:], io["pick"]).then_inc(sem["b_small"], 16)
            sp.dma_start(mem["wu"][:], io["wu"]).then_inc(sem["b_small"], 16)
            sp.dma_start(mem["bias_u"][:], io["bu"]).then_inc(sem["b_small"], 16)

            def load(n):
                for to, loads, loaded in ((mem["k_raw"][:, n.at % 2], LOADS[0], sem[f"k_loaded{n.at % 2}"]),
                                          (qq[:, n.at % NBUF], LOADS[1], sem[f"q_loaded{n.at % NBUF}"])):
                    for row, part, many in loads:
                        src = io["q_parts"][part:part + many].rearrange("c (d j) t -> (c d) j t", j=NJ)
                        sp.dma_start(to[row * HD:(row + many) * HD], src[:, :, bass.ds(n.number() * AT, AT)]).then_inc(loaded, 16)

            def shift_rows(n):
                cols = bass.ds(n.number() * AT, AT)
                wait_alone(sp, sem["shift_work"], 3 * (n.number() + 1), sem["sp_passed"])
                for c in range(CHUNKS):
                    for part in range(3):
                        to = io["shift_rows"][part, c * JC:(c + 1) * JC, cols].rearrange("j (b t) -> b j t", t=HEAD_TOK)
                        sp.dma_start(to, shift_part[c * NB:(c + 1) * NB, n.at % 2, part].rearrange("b (j t) -> b j t", t=HEAD_TOK)
                                     ).then_inc(sem["shift_stored"], 16)
                wait_alone(sp, sem["shift_stored"], SHIFT_DMAS * (n.number() + 1), sem["sp_passed"])
                sp.dma_start(qq[ROWS:ROWS + 3, n.at % NBUF], io["shift_rows"][:, :, cols]).then_inc(sem[f"shift_set{n.at % 2}"], 16)

            def step(t):
                n = t + 3
                if n.exists():
                    if t.past(1):
                        wait_alone(sp, sem["exp_mm"], NB * t.number(), sem["sp_passed"])
                    if n.past(2):
                        wait_alone(sp, sem["keys_ready"], COLG * (t.number() + 2), sem["sp_passed"])
                    load(n)
                if (t + 1).exists():
                    shift_rows(t + 1)
                n = t + -2
                if n.exists():
                    wait_alone(sp, sem["y_done"], Y_FREE + n.number() + 1, sem["sp_passed"])
                    cols = bass.ds(n.number() * AT, AT)
                    sp.dma_start(io["out"][:, cols], y_sum[:, cols]).then_inc(sem["y_stored"], 16)

            load(Tile(0, 0))
            steps(sp, step)
            wait_alone(sp, sem["y_stored"], 16 * A_TILES, sem["sp_passed"])

        @block.gpsimd
        def _(pool):
            pool.memset(qk[32:64].rearrange("p n b c -> p (n b c)"), 1.0).then_inc(sem["ones_set"], 1)
            wait_alone(pool, sem["ones_set"], 1, sem["pool_passed"])
            pool.memset(v_aug[:].rearrange("p n c v -> p (n c v)"), 0.0).then_inc(sem["v_set"], 1)
            wait_alone(pool, sem["v_set"], 1, sem["pool_passed"])
            pool.memset(v_aug[:, :, :, HD:2 * HD], 1.0).then_inc(sem["v_set"], 1)

            def shift_rows(n):
                b, done = n.at % 2, 3 * n.number()
                wait_alone(pool, sem["shift_first"], n.number() + 1, sem["pool_passed"])
                nc.gpsimd.tensor_tensor(shift_rest[:], neg_max[:], shift_part[:, b, 0], ALU.subtract).then_inc(sem["shift_work"], 1)
                wait_alone(pool, sem["shift_work"], done + 1, sem["pool_passed"])
                nc.gpsimd.tensor_copy(shift_part[:, b, 1], shift_rest[:]).then_inc(sem["shift_work"], 1)
                wait_alone(pool, sem["shift_work"], done + 2, sem["pool_passed"])
                nc.gpsimd.tensor_tensor(shift_part[:, b, 2], shift_rest[:], shift_part[:, b, 1], ALU.subtract).then_inc(sem["shift_work"], 1)

            def to_features(n):
                b = n.at % 2
                wait_alone(pool, sem["pv_out"], PV_FREE + GROUPS * (n.number() + 1), sem["pool_passed"])
                for c in range(COLG):
                    to = io["o_rows"][:, :, bass.ds(n.number() * AT + c * GROUPS * HEAD_TOK, GROUPS * HEAD_TOK)]
                    src = o_stage[PV_ROWS * c:PV_ROWS * c + 2 * HD, b].rearrange("p j s t -> p j (s t)")
                    pool.dma_start(to, src).then_inc(sem[f"o_written{b}"], 16)
                wait_alone(pool, sem[f"o_written{b}"], STAGE_DMAS * (n.laps(2) + 1), sem["pool_passed"])
                wait_alone(pool, sem["projected"], PROJ_FREE + n.number() - 1, sem["pool_passed"])
                cols = bass.ds(n.number() * AT, AT)
                pool.dma_start(o_feat[:, b], io["o_rows"].rearrange("(w d) j t -> (d j) w t", w=2)[:, :, cols]).then_inc(sem[f"o_read{b}"], 16)

            def step(t):
                if (t + 1).exists():
                    shift_rows(t + 1)
                if (t + -1).exists():
                    to_features(t + -1)

            steps(pool, step)

        @block.vector
        def _(dve):
            dve.sem_inc(sem["max_done"], MAX_FREE)
            dve.sem_inc(sem["y_done"], Y_FREE)
            dve.wait_ge(sem["b_small"], 3 * 16)
            dve.wait_ge(sem["ones_set"], 1)

            def keys_in_order(n, part):
                if part == 0:
                    dve.wait_ge(sem[f"k_loaded{n.at % 2}"], KEYS_LOADED * (n.laps(2) + 1))
                    if n.past(4):
                        dve.wait_ge(sem["exp_mm"], NB * (n.number() - 3))
                bs = slice(part * NB // 4, (part + 1) * NB // 4)
                src = mem["k_raw"][:, n.at % 2].rearrange("p j (b t) -> p b j t", t=HEAD_TOK)[:, bs]
                nc.vector.tensor_copy(qk[0:ROWS, n.at % NBUF, bs].rearrange("p b (j t) -> p b j t", t=HEAD_TOK), src).then_inc(sem["keys_ready"], 1)

            for part in range(4):
                keys_in_order(Tile(0, 0), part)

            def step(t):
                n, old = t + 2, t + -2
                b = old.at % 2
                for k in range(NB):
                    if n.exists():
                        at = block_of(k)
                        dve.wait_ge(sem["max_mm"], NB * n.number() + k + 1)
                        nc.vector.tensor_reduce(out=row_max[:, n.at % 2, :, at], in_=ps_max[:, k % 2].rearrange("p (c q) -> p c q", q=POS),
                                                axis=AX.X, op=ALU.max).then_inc(sem["max_done"], 1)
                    if k >= 9 and k % 2 and (t + 3).exists():
                        keys_in_order(t + 3, (k - 9) // 2)
                    if old.exists() and k == 3:
                        dve.wait_ge(sem[f"o_read{b}"], 16 * (old.laps(2) + 1))
                        nc.vector.reciprocal(o_feat[:, b, 1], o_feat[:, b, 1]).then_inc(sem["sum_inverted"], 1)
                    if old.exists() and k == 5:
                        dve.wait_ge(sem["sum_inverted"], old.number() + 1)
                        nc.vector.tensor_tensor(o_feat[:, b, 0], o_feat[:, b, 0], o_feat[:, b, 1], ALU.mult).then_inc(sem["o_normed"], 1)
                    if old.exists() and k == 11:
                        dve.wait_ge(sem["projected"], PROJ_FREE + old.number() + 1)
                        to = y_sum[:, bass.ds(old.number() * AT, AT)]
                        nc.vector.scalar_tensor_tensor(out=to, in0=ps_misc[:, (t.at + 1) % 2, 0:AT], scalar=mem["bias_u"][:, 0:1], in1=to,
                                                       op0=ALU.add, op1=ALU.add).then_inc(sem["y_done"], 1)

            steps(dve, step)

        @block.scalar
        def _(act):
            act.sem_inc(sem["exp_done"], EXP_FREE)
            act.sem_inc(sem["pv_out"], PV_FREE)
            act.wait_ge(sem["v_set"], 2)

            def values_out(n):
                act.wait_ge(sem["max_mm"], NB * (n.number() + 1))
                src = ps_misc[:, n.at % 2, 0:NB * CHUNKS * HD].rearrange("p (c v) -> p c v", v=HD)
                nc.scalar.activation(v_aug[:, n.at % NBUF, :, 0:HD], src, ACT.Copy).then_inc(sem["v_done"], 1)

            def shift_out(n):
                b = n.at % 2
                act.wait_ge(sem["max_turned"], n.number() + 1)
                if n.past(1):
                    act.wait_ge(sem["shift_work"], 3 * n.number())
                if n.past(2):
                    act.wait_ge(sem["shift_stored"], SHIFT_DMAS * (n.number() - 1))
                src = ps_misc[0:CHUNKS * NB, (n.at + 0) % 2, 0:P]
                nc.scalar.activation(neg_max[:], src, ACT.Copy, scale=-1.0)
                nc.scalar.activation(shift_part[:, b, 0], src, ACT.Copy, scale=-1.0).then_inc(sem["shift_first"], 1)

            def pv_out(n, s):
                done = GROUPS * n.number() + s
                act.wait_ge(sem["pv_mm"], PV_FREE + done + 1)
                if s == 0 and n.past(2):
                    act.wait_ge(sem[f"o_written{n.at % 2}"], STAGE_DMAS * n.laps(2))
                nc.scalar.activation(o_stage[:, n.at % 2, :, s], ps_pv[:, s % 2, 0:POS].rearrange("p (j t) -> p j t", t=HEAD_TOK),
                                     ACT.Copy).then_inc(sem["pv_out"], 1)

            def step(t):
                for k in range(NB):
                    s = k // COLG
                    if t.exists():
                        act.wait_ge(sem["exp_mm"], NB * t.number() + k + 1)
                        if k % COLG == 0:
                            act.wait_ge(sem["pv_mm"], PV_FREE + GROUPS * t.number() + s - 1)
                        nc.scalar.activation(probs[:, k % (2 * COLG)], ps_exp[:, k % 2], ACT.Exp, scale=SCORE_SCALE).then_inc(sem["exp_done"], 1)
                    if k == 0 and (t + 1).exists():
                        values_out(t + 1)
                    if k == 5 and (t + 1).exists():
                        shift_out(t + 1)
                    if k % COLG == COLG - 1:
                        n = t if s else t + -1
                        if n.exists():
                            pv_out(n, (s - 1) % GROUPS)

            steps(act, step)

        @block.tensor
        def _(pe):
            pe.sem_inc(sem["pv_mm"], PV_FREE)
            pe.sem_inc(sem["projected"], PROJ_FREE)
            pe.wait_ge(sem["b_small"], 3 * 16)
            pe.wait_ge(sem["ones_set"], 1)

            def keys(n, k, c, rows):
                return qk[0:rows, n.at % NBUF, block_of(k), c * P:(c + 1) * P]

            def queries(n, k, rows):
                at = block_of(k) * HEAD_TOK
                return qq[0:rows, n.at % NBUF, :, at:at + HEAD_TOK]

            def scores(n, k, rows, bank, values=None):
                for c in range(CHUNKS):
                    if values is not None:
                        col = (CHUNKS * k + c) * HD
                        nc.tensor.matmul(values[:, col:col + HD], keys(n, k, c, ROWS), mem["pick"][:], start=True, stop=True)
                    last = nc.tensor.matmul(bank[:, c * POS:(c + 1) * POS], keys(n, k, c, rows), queries(n, k, rows), start=True, stop=True)
                return last

            def weighted_values(n, s, c):
                done = GROUPS * n.number() + s
                if c == 0:
                    pe.wait_ge(sem["exp_done"], EXP_FREE + COLG * (done + 1))
                    pe.wait_ge(sem["pv_out"], PV_FREE + done - 1)
                    if s == 0:
                        pe.wait_ge(sem["v_done"], n.number() + 1)
                for g in range(COLG):
                    k = COLG * s + g
                    last = nc.tensor.matmul(ps_pv[PV_ROWS * g:PV_ROWS * (g + 1), s % 2, 0:POS], v_aug[:, n.at % NBUF, CHUNKS * k + c],
                                            probs[:, k % (2 * COLG), c * POS:(c + 1) * POS], start=(c == 0), stop=(c == CHUNKS - 1))
                if c == CHUNKS - 1:
                    last.then_inc(sem["pv_mm"], 1)

            def step(t):
                n, old = t + 2, t + -2
                for k in range(NB):
                    s = k // COLG
                    if n.exists():
                        if k == 0:
                            pe.wait_ge(sem["keys_ready"], COLG * (n.number() + 1))
                            pe.wait_ge(sem[f"q_loaded{n.at % NBUF}"], QUERIES_LOADED * (n.laps(NBUF) + 1))
                            if t.past(0):
                                pe.wait_ge(sem["shift_first"], t.number() + 1)
                            if t.past(3):
                                pe.wait_ge(sem["y_done"], Y_FREE + t.number() - 2)
                        pe.wait_ge(sem["max_done"], MAX_FREE + NB * n.number() + k - 1)
                        scores(n, k, ROWS, ps_max[:, k % 2], ps_misc[:, n.at % 2]).then_inc(sem["max_mm"], 1)
                    if k == 4 and (t + 1).exists():
                        pe.wait_ge(sem["max_done"], MAX_FREE + NB * (t.number() + 2))
                        pe.wait_ge(sem["v_done"], t.number() + 2)
                        nc.tensor.transpose(ps_misc[0:CHUNKS * NB, (t.at + 1) % 2, 0:P],
                                            row_max[:, (t.at + 1) % 2].rearrange("p c b -> p (c b)"), mem["ident"][:]).then_inc(sem["max_turned"], 1)
                    if t.exists():
                        if k == 0:
                            pe.wait_ge(sem[f"shift_set{t.at % 2}"], 16 * (t.laps(2) + 1))
                        pe.wait_ge(sem["exp_done"], EXP_FREE + NB * t.number() + k - 1)
                        scores(t, k, ROWS + 3, ps_exp[:, k % 2]).then_inc(sem["exp_mm"], 1)
                    if k == 9 and old.exists():
                        pe.wait_ge(sem["o_normed"], old.number() + 1)
                        if (t + 1).exists():
                            pe.wait_ge(sem["shift_first"], t.number() + 2)
                        nc.tensor.matmul(ps_misc[:, (t.at + 1) % 2, 0:AT], mem["wu"][:], o_feat[:, old.at % 2, 0], start=True, stop=True
                                         ).then_inc(sem["projected"], 1)
                    if k % 2 == 1:
                        m = t if s else t + -1
                        if m.exists():
                            weighted_values(m, (s - 1) % GROUPS, (k % COLG) // 2)

            steps(pe, step)


B_SEMS = ("b_small ones_set v_set k_loaded0 k_loaded1 keys_ready q_loaded0 q_loaded1 q_loaded2 q_loaded3 max_mm max_done max_turned shift_first shift_work "
          "shift_stored shift_set0 shift_set1 exp_mm exp_done pv_mm pv_out v_done o_written0 o_written1 o_read0 o_read1 sum_inverted "
          "o_normed projected y_done y_stored").split()

INPUTS = ("x xT w1 w2 h1 h2 w3 wq wu w1s w2s h1s h2s w3s bq bu ident pick").split()


def build(nc, arrays):
    io = {n: nc.dram_tensor(f"in_{n}", arrays[f"in_{n}"].shape, mybir.dt.from_np(arrays[f"in_{n}"].dtype), kind="ExternalInput").ap()
          for n in INPUTS}
    io["out"] = nc.dram_tensor("out_T", (EMB, TOKENS), F32, kind="ExternalOutput").ap()
    io["q_parts"] = nc.dram_tensor("q_parts", (3, EMB, TOKENS), BF16, kind="Internal").ap()
    io["o_rows"] = nc.dram_tensor("o_rows", (2 * HD, NJ, TOKENS), F32, kind="Internal").ap()
    io["shift_rows"] = nc.dram_tensor("shift_rows", (3, NJ, TOKENS), BF16, kind="Internal").ap()
    with ExitStack() as both:
        def sbuf(stack, name, shape, dtype=F32):
            mem[name] = stack.enter_context(nc.sbuf_tensor(name, shape, dtype))

        def psum(stack, name, shape):
            mem[name] = stack.enter_context(nc.psum_tensor(name, shape, F32))

        mem = {}
        sbuf(both, "y_sum", [P, TOKENS])
        sbuf(both, "ident", [P, P])
        sem = {n: both.enter_context(nc.semaphore(n)) for n in FF_SEMS + B_SEMS}
        with ExitStack() as a:
            for name, shape, dtype in (
                    ("w_hi", [P, WCOLS], F32R), ("w_lo", [P, WCOLS], F32R), ("h_hi", [P, 2, 2, KB, TT], F32R), ("h_lo", [P, 2, 2, KB, TT], F32R),
                    ("hf", [P, HF_RING, TT], F32), ("silu_out", [P, 2, TT], F32), ("x_nat", [P, 2, SUB, P], F32), ("xn_nat", [P, 2, SUB, P], F32),
                    ("xn_hi", [P, 2, TT], F32R), ("xn_lo", [P, 2, TT], F32R), ("q_full", [P, 2, TT], F32), ("q_rest", [P, 2, TT], F32),
                    ("q_part", [P, 2, 3, TT], BF16), ("stats", [P, 2 * SUB, 6], F32), ("moments", [P, 2 * SUB, 2], F32),
                    ("var_eps", [P, 2 * SUB], F32), ("rstd", [P, 2 * SUB], F32), ("minus_half", [P, 2 * SUB], F32),
                    ("scales", [P, 4 * KB + 1], F32), ("bias_q", [P, 1], F32), ("ones", [P, 1], F32), ("lo_max", [P, 1], F32), ("flag", [1, 1], I32)):
                sbuf(a, name, shape, dtype)
            psum(a, "ps_ff", [P, FF_SLOTS, 2, TT])
            psum(a, "ps_prep", [P, 2, TT])
            feed_forward(nc, io, mem, sem)
        with ExitStack() as b:
            for name, shape, dtype in (
                    ("qk", [64, NBUF, NB, POS], BF16), ("k_raw", [ROWS, 2, NJ, AT], BF16), ("qq", [64, NBUF, NJ, AT], BF16), ("v_aug", [P, NBUF, NB * CHUNKS, PV_ROWS], F32),
                    ("probs", [P, 2 * COLG, CHUNKS * POS], F32), ("row_max", [P, 2, CHUNKS, NB], F32), ("neg_max", [CHUNKS * NB, P], F32),
                    ("shift_rest", [CHUNKS * NB, P], F32), ("shift_part", [CHUNKS * NB, 2, 3, P], BF16), ("o_stage", [P, 2, NJ, GROUPS, HEAD_TOK], F32),
                    ("o_feat", [P, 2, 2, AT], F32), ("wu", [P, P], F32), ("bias_u", [P, 1], F32), ("pick", [ROWS, HD], BF16)):
                sbuf(b, name, shape, dtype)
            psum(b, "ps_max", [P, 2, 512])
            psum(b, "ps_exp", [P, 2, 512])
            psum(b, "ps_pv", [P, 2, 512])
            psum(b, "ps_misc", [P, 2, 512])
            attention(nc, io, mem, sem)


def kernel(L0_attn_x, L0_attn_wq, L0_attn_bq, L0_attn_wu, L0_attn_bu, L0_ffn_w1_w, L0_ffn_w1_s, L0_ffn_w2_w, L0_ffn_w2_s,
           L0_ffn_h1_w, L0_ffn_h1_s, L0_ffn_h2_w, L0_ffn_h2_s, L0_ffn_w3_w, L0_ffn_w3_s):
    import concourse.bacc as bacc
    import ml_dtypes
    from concourse.bass_utils import run_bass_kernel_spmd

    def laid(a):
        return np.ascontiguousarray(np.asarray(a))

    x = laid(L0_attn_x).reshape(TOKENS, EMB)
    order = np.arange(EMB).reshape(NJ, HD).T.ravel()
    pick = np.zeros((ROWS, HD), ml_dtypes.bfloat16)
    for block, part in enumerate(PARTS_OF_KEYS):
        if part not in PARTS_OF_KEYS[:block]:
            pick[block * HD + np.arange(HD), np.arange(HD)] = 1
    columns = lambda s: laid(np.asarray(s).reshape(-1, P).T)
    arrays = {
        "in_x": x, "in_xT": laid(x.T),
        "in_w1": laid(np.asarray(L0_ffn_w1_w).T), "in_w2": laid(np.asarray(L0_ffn_w2_w).T),
        "in_h1": laid(np.asarray(L0_ffn_h1_w).T), "in_h2": laid(np.asarray(L0_ffn_h2_w).T), "in_w3": laid(np.asarray(L0_ffn_w3_w).T),
        "in_wq": laid(np.asarray(L0_attn_wq)[order].T), "in_wu": laid(np.asarray(L0_attn_wu).T[order]),
        "in_w1s": columns(L0_ffn_w1_s), "in_w2s": columns(L0_ffn_w2_s), "in_h1s": columns(L0_ffn_h1_s), "in_h2s": columns(L0_ffn_h2_s),
        "in_w3s": columns(L0_ffn_w3_s), "in_bq": columns(np.asarray(L0_attn_bq)[order]), "in_bu": columns(L0_attn_bu),
        "in_ident": np.eye(P, dtype=np.float32), "in_pick": pick,
    }
    nc = bacc.Bacc("TRN2", target_bir_lowering=False, num_devices=1)
    build(nc, arrays)
    result = run_bass_kernel_spmd(nc, [arrays], core_ids=[0])
    return laid(result.results[0]["out_T"].T).reshape(BATCH, SEQ, EMB)
```

```python
from contextlib import ExitStack

import numpy as np
import concourse.bass as bass
from concourse import mybir
from concourse.alu_op_type import AluOpType as ALU

F32 = mybir.dt.float32
F32R = mybir.dt.float32r
BF16 = mybir.dt.bfloat16
I32 = mybir.dt.int32
ACT = mybir.ActivationFunctionType
AX = mybir.AxisListType

BATCH, SEQ, EMB, HID = 32, 256, 128, 512
TOKENS = BATCH * SEQ
P = 128
HEADS = 16
HD = EMB // HEADS
NJ = EMB // HD
HEAD_TOK = SEQ // NJ
POS = SEQ
EPS = 1e-5
SCORE_SCALE = 1.0 / float(np.sqrt(EMB))

TT = 512
SUB = TT // P
KB = HID // P
PAIRS = TOKENS // (2 * TT)
HF_RING = 4
OPS = 3 * 2 * KB
FF_SLOTS = 3

W1, W2, H1, H2 = 0, HID, 2 * HID, (2 + KB) * HID
W3 = H2 + KB * HID
WQ = W3 + KB * P
WCOLS = WQ + P

AT = 256
NB = AT // HEAD_TOK
A_TILES = TOKENS // AT
COLG = 4
GROUPS = NB // COLG
NBUF = 4
CHUNKS = POS // P
ROWS = 6 * HD
SHIFT_AT = 96
SHIFT_PARTS = 2
PARTS_OF_KEYS, PARTS_OF_QUERIES = (0, 0, 0, 1, 1, 2), (0, 1, 2, 0, 1, 0)
PV_ROWS = 32
LOADS = ((0, 0, 1), (1, 0, 1), (2, 0, 2), (4, 1, 2)), ((0, 0, 3), (3, 0, 2), (5, 0, 1))
KEYS_LOADED, QUERIES_LOADED = 16 * len(LOADS[0]), 16 * len(LOADS[1])


def block_of(k):
    return COLG * (k % COLG) + k // COLG


def wait_alone(engine, semaphore, value, passed):
    engine.wait_ge(semaphore, value)
    engine.sem_inc(passed, 1)


def feed_forward(nc, io, mem, sem):
    ps_ff, ps_prep = mem["ps_ff"], mem["ps_prep"]
    w_hi, w_lo, h_hi, h_lo = mem["w_hi"], mem["w_lo"], mem["h_hi"], mem["h_lo"]
    hf, silu_out, y_sum = mem["hf"], mem["silu_out"], mem["y_sum"]
    x_nat, xn_nat, xn_hi, xn_lo = mem["x_nat"], mem["xn_nat"], mem["xn_hi"], mem["xn_lo"]
    q_full, q_rest, q_part = mem["q_full"], mem["q_rest"], mem["q_part"]
    stats, moments, var_eps, rstd = mem["stats"], mem["moments"], mem["var_eps"], mem["rstd"]
    scales, bias_q = mem["scales"], mem["bias_q"]
    FREE = 2

    def slot_is_free(pe, p, j):
        before, pair = (j - FF_SLOTS, p) if j >= FF_SLOTS else (j - FF_SLOTS + 18, p - 1)
        if before < 8:
            pe.wait_ge(sem["gated"], FREE + 8 * pair + before + 1)
        elif before < 16:
            pe.wait_ge(sem["gelu_full"], 16 + 16 * pair + 2 * (before - 8) + 2)
        else:
            pe.wait_ge(sem["ff_added"], FREE + 2 * pair + before - 16 + 1)

    def h_ready(pe, p, k):
        pe.wait_ge(sem["h_hi_done"], HF_RING + OPS * p + k)
        pe.wait_ge(sem["h_lo_done"], HF_RING + OPS * p + k)

    with nc.Block() as block:
        @block.sync
        def _(sp):
            def load_x(u, pair, first):
                if not first:
                    wait_alone(sp, sem["sub_normed"], 2 * SUB * pair, sem["sp_passed"])
                src = io["x"].rearrange("(n s p) e -> p n s e", p=P, s=SUB)
                if first:
                    src = src[:, u]
                else:
                    src = src[:, bass.ds(2 * pair + u, 1)].rearrange("p o s e -> p (o s) e")
                sp.dma_start(x_nat[:, u], src).then_inc(sem[f"x_loaded{u}"], 16)

            for u in range(2):
                load_x(u, 0, True)
            staged = y_sum[:, TOKENS - WCOLS:]
            for n, (name, at, blocks, cols) in enumerate((("w1", W1, 1, HID), ("w2", W2, 1, HID), ("h1", H1, KB, HID),
                                                          ("h2", H2, KB, HID), ("w3", W3, KB, P), ("wq", WQ, 1, P))):
                to = staged[:, at:at + blocks * cols].rearrange("p (b c) -> p b c", c=cols)
                sp.dma_start(to, io[name].rearrange("(b p) c -> p b c", p=P)).then_inc(sem["w_loaded"], 16)
            wait_alone(sp, sem["w_split"], 2, sem["sp_passed"])
            half = TOKENS // 2
            sp.dma_start(y_sum[:, half:], io["xT"][:, half:]).then_inc(sem["xT_loaded"], 16)

            def store_q(u, pair):
                wait_alone(sp, sem["q_third"], 2 * pair + u + 1, sem["sp_passed"])
                to = io["q_parts"][:, :, bass.ds((2 * pair + u) * TT, TT)].rearrange("c f t -> f c t")
                sp.dma_start(to, q_part[:, u]).then_inc(sem[f"q_stored{u}"], 16)

            for u in range(2):
                store_q(u, 0)
            with sp.Fori(0, PAIRS - 1) as p:
                for u in range(2):
                    load_x(u, p + 1, False)
                for u in range(2):
                    store_q(u, p + 1)
            for u in range(2):
                wait_alone(sp, sem[f"q_stored{u}"], 16 + 16 * PAIRS, sem["sp_passed"])

        @block.gpsimd
        def _(pool):
            pool.dma_start(mem["ident"][:], io["ident"]).then_inc(sem["small_loaded"], 16)
            for n, name in enumerate(("w1s", "w2s", "h1s", "h2s")):
                pool.dma_start(scales[:, n * KB:(n + 1) * KB], io[name]).then_inc(sem["small_loaded"], 16)
            pool.dma_start(scales[:, 4 * KB:4 * KB + 1], io["w3s"]).then_inc(sem["small_loaded"], 16)
            pool.dma_start(bias_q[:], io["bq"]).then_inc(sem["small_loaded"], 16)
            pool.dma_start(y_sum[:, :TOKENS // 4], io["xT"][:, :TOKENS // 4]).then_inc(sem["xT_first"], 16)
            wait_alone(pool, sem["w_split"], 2, sem["pool_passed"])
            pool.dma_start(y_sum[:, TOKENS // 4:TOKENS // 2], io["xT"][:, TOKENS // 4:TOKENS // 2]).then_inc(sem["xT_second"], 16)
            pool.memset(mem["minus_half"][:], -0.5).then_inc(sem["const_set"], 1)
            wait_alone(pool, sem["const_set"], 1, sem["pool_passed"])

            def inverse_deviation(pair):
                wait_alone(pool, sem["var_ready"], pair + 1, sem["pool_passed"])
                nc.gpsimd.tensor_tensor(rstd[:], var_eps[:], mem["minus_half"][:], ALU.pow).then_inc(sem["rstd_ready"], 1)

            def q_remainders(pair):
                for u in range(2):
                    wait_alone(pool, sem["q_first"], 2 * pair + u + 1, sem["pool_passed"])
                    nc.gpsimd.tensor_tensor(q_rest[:, u], q_full[:, u], q_part[:, u, 0], ALU.subtract).then_inc(sem["q_rest_ready"], 1)
                for u in range(2):
                    wait_alone(pool, sem["q_second"], 2 * pair + u + 1, sem["pool_passed"])
                    nc.gpsimd.tensor_tensor(q_part[:, u, 2], q_rest[:, u], q_part[:, u, 1], ALU.subtract).then_inc(sem["q_third"], 1)

            inverse_deviation(0)
            q_remainders(0)
            with pool.Fori(0, PAIRS - 1) as p:
                inverse_deviation(p + 1)
                q_remainders(p + 1)

        @block.vector
        def _(dve):
            staged = y_sum[:, TOKENS - WCOLS:]
            dve.sem_inc(sem["gated"], FREE)
            dve.sem_inc(sem["ff_added"], FREE)
            dve.sem_inc(sem["h_lo_done"], HF_RING)
            dve.memset(mem["ones"][:], 1.0).then_inc(sem["const_set"], 2)
            dve.wait_ge(sem["w_loaded"], 6 * 16)
            dve.wait_ge(sem["w_hi_done"], 1)
            nc.vector.tensor_tensor(w_lo[:], staged, w_hi[:].bitcast(F32), ALU.subtract).then_inc(sem["w_split"], 2)
            dve.wait_ge(sem["w_split"], 2)
            nc.vector.tensor_reduce(out=mem["lo_max"][:], in_=w_lo[:, :WQ].bitcast(F32), axis=AX.X, op=ALU.max,
                                    apply_absolute_value=True).then_inc(sem["lo_max_ready"], 1)
            dve.wait_ge(sem["lo_sum_ready"], 1)
            nc.vector.tensor_scalar(mem["flag"][:], ps_prep[0:1, 0, 0:1], 0.0, None, ALU.not_equal).then_inc(sem["flag_ready"], 1)

            def norm_inputs(pair):
                for u in range(2):
                    dve.wait_ge(sem[f"x_loaded{u}"], 16 * (pair + 1))
                    for s in range(SUB):
                        nc.vector.bn_stats(out=stats[:, u * SUB + s], in_=x_nat[:, u, s]).then_inc(sem["stats_done"], 1)
                for n in range(2 * SUB):
                    if n == 0:
                        wait_alone(dve, sem["stats_done"], 2 * SUB * (pair + 1), sem["dve_passed"])
                    nc.vector.bn_aggr(out=moments[:, n], in_=stats[:, n]).then_inc(sem["moments_done"], 1)
                dve.wait_ge(sem["moments_done"], 2 * SUB * (pair + 1))
                nc.vector.tensor_scalar(var_eps[:], moments[:, :, 1], EPS, None, ALU.add).then_inc(sem["var_ready"], 1)
                dve.wait_ge(sem["rstd_ready"], pair + 1)
                dve.wait_ge(sem["transposed"], 2 + 2 * pair)
                for n in range(2 * SUB):
                    u, s = n // SUB, n % SUB
                    nc.vector.tensor_scalar(xn_nat[:, u, s], x_nat[:, u, s], moments[:, n, 0:1], rstd[:, n:n + 1],
                                            ALU.subtract, ALU.mult).then_inc(sem["sub_normed"], 1)

            def lo_part(p, k, layer, u, b):
                if layer == 0:
                    dve.wait_ge(sem["gated"], FREE + 8 * p + k + 1)
                else:
                    dve.wait_ge(sem["gelu_full"], 16 + 16 * p + (k - 8) + 1)
                dve.wait_ge(sem["h_hi_done"], HF_RING + OPS * p + k + 1)
                nc.vector.tensor_tensor(h_lo[:, layer % 2, u, b], hf[:, k % HF_RING], h_hi[:, layer % 2, u, b].bitcast(F32),
                                        ALU.subtract).then_inc(sem["h_lo_done"], 1)

            def xn_low(pair):
                for u in range(2):
                    dve.wait_ge(sem["xn_hi_done"], 2 * pair + u + 1)
                    nc.vector.tensor_tensor(xn_lo[:, u], ps_prep[:, u], xn_hi[:, u].bitcast(F32), ALU.subtract).then_inc(sem["xn_lo_done"], 1)

            def pair_of_tiles(p, more):
                for u in range(2):
                    for b in range(KB):
                        k, slot = KB * u + b, (KB * u + b) % FF_SLOTS
                        dve.wait_ge(sem["silu_done"], FREE + 8 * p + k + 1)
                        dve.wait_ge(sem["h_hi_done"], OPS * p + k + 1)
                        dve.wait_ge(sem["h_lo_done"], OPS * p + k + 1)
                        nc.vector.scalar_tensor_tensor(out=hf[:, k % HF_RING], in0=ps_ff[:, slot, 1], scalar=scales[:, KB + b:KB + b + 1],
                                                       in1=silu_out[:, k % 2], op0=ALU.mult, op1=ALU.mult).then_inc(sem["gated"], 1)
                        lo_part(p, k, 0, u, b)
                if more:
                    norm_inputs(p + 1)
                for u in range(2):
                    for b in range(KB):
                        lo_part(p, 8 + KB * u + b, 1, u, b)
                if more:
                    xn_low(p + 1)
                for u in range(2):
                    for b in range(KB):
                        lo_part(p, 16 + KB * u + b, 2, u, b)
                if more:
                    q_seconds(p + 1)
                for u in range(2):
                    slot = (16 + u) % FF_SLOTS
                    dve.wait_ge(sem["down_done"], 2 * p + u + 1)
                    to = y_sum[:, bass.ds((2 * p + u) * TT, TT)]
                    nc.vector.scalar_tensor_tensor(out=to, in0=ps_ff[:, slot, 0], scalar=scales[:, 4 * KB:4 * KB + 1], in1=to,
                                                   op0=ALU.mult, op1=ALU.add).then_inc(sem["ff_added"], 1)

            def q_seconds(pair):
                for u in range(2):
                    dve.wait_ge(sem["q_rest_ready"], 2 * pair + u + 1)
                    nc.vector.tensor_copy(q_part[:, u, 1], q_rest[:, u]).then_inc(sem["q_second"], 1)

            norm_inputs(0)
            xn_low(0)
            q_seconds(0)
            dve.wait_ge(sem["small_loaded"], 7 * 16)
            dve.wait_ge(sem["xT_first"], 16)
            dve.wait_ge(sem["xT_second"], 16)
            dve.wait_ge(sem["xT_loaded"], 16)
            with dve.Fori(0, PAIRS - 1) as p:
                pair_of_tiles(p, True)
            pair_of_tiles(PAIRS - 1, False)

        @block.scalar
        def _(act):
            act.sem_inc(sem["gelu_full"], 16)
            act.sem_inc(sem["h_hi_done"], HF_RING)
            act.sem_inc(sem["silu_done"], FREE)
            for u in range(2):
                act.sem_inc(sem[f"q_stored{u}"], 16)
            act.wait_ge(sem["w_loaded"], 6 * 16)
            nc.scalar.activation(w_hi[:], y_sum[:, TOKENS - WCOLS:], ACT.Identity).then_inc(sem["w_hi_done"], 1)
            act.wait_ge(sem["small_loaded"], 7 * 16)

            def xn_high(pair):
                for u in range(2):
                    act.wait_ge(sem["transposed"], 2 + 2 * pair + u + 1)
                    nc.scalar.activation(xn_hi[:, u], ps_prep[:, u], ACT.Identity).then_inc(sem["xn_hi_done"], 1)

            def q_out(pair):
                for u in range(2):
                    act.wait_ge(sem["q_product"], 2 * pair + u + 1)
                    act.wait_ge(sem[f"q_stored{u}"], 16 + 16 * pair)
                    nc.scalar.activation(q_full[:, u], ps_prep[:, u], ACT.Identity, bias=bias_q[:, 0:1])
                    nc.scalar.activation(q_part[:, u, 0], ps_prep[:, u], ACT.Identity, bias=bias_q[:, 0:1]).then_inc(sem["q_first"], 1)

            def silu(p, k):
                act.wait_ge(sem["up_done"], 8 * p + k + 1)
                act.wait_ge(sem["gated"], 8 * p + k + 1)
                nc.scalar.activation(silu_out[:, k % 2], ps_ff[:, k % FF_SLOTS, 0], ACT.Silu, scale=scales[:, k % KB:k % KB + 1]).then_inc(sem["silu_done"], 1)

            def high_copy(p, k):
                act.wait_ge(sem["gated"], FREE + 8 * p + k + 1)
                nc.scalar.activation(h_hi[:, 0, k // KB, k % KB], hf[:, k % HF_RING], ACT.Identity).then_inc(sem["h_hi_done"], 1)

            def gelu(p, layer, u, b):
                k = 8 * layer + KB * u + b
                slot = 8 + (k - 8) // 2
                src = ps_ff[:, slot % FF_SLOTS, b % 2]
                s = scales[:, (1 + layer) * KB + b:(1 + layer) * KB + b + 1]
                act.wait_ge(sem["hidden_done"], 16 * p + (k - 8) + 1)
                nc.scalar.activation(h_hi[:, layer % 2, u, b], src, ACT.Gelu, scale=s).then_inc(sem["h_hi_done"], 1)
                act.wait_ge(sem["h_lo_done"], OPS * p + k + 1)
                act.wait_ge(sem["h_hi_done"], OPS * p + k + 1)
                nc.scalar.activation(hf[:, k % HF_RING], src, ACT.Gelu, scale=s).then_inc(sem["gelu_full"], 1)

            def pair_of_tiles(p, more):
                silu(p, 0)
                for k in range(1, 2 * KB):
                    silu(p, k)
                    high_copy(p, k - 1)
                high_copy(p, 2 * KB - 1)
                for u in range(2):
                    for b in range(KB):
                        gelu(p, 1, u, b)
                if more:
                    xn_high(p + 1)
                for u in range(2):
                    for b in range(KB):
                        gelu(p, 2, u, b)
                    if more and u == 0:
                        q_out(p + 1)

            xn_high(0)
            q_out(0)
            with act.Fori(0, PAIRS - 1) as p:
                pair_of_tiles(p, True)
            pair_of_tiles(PAIRS - 1, False)

        @block.tensor
        def _(pe):
            pe.sem_inc(sem["transposed"], 2)
            pe.wait_ge(sem["lo_max_ready"], 1)
            pe.wait_ge(sem["const_set"], 3)
            nc.tensor.matmul(ps_prep[0:1, 0, 0:1], mem["lo_max"][:], mem["ones"][:], start=True, stop=True).then_inc(sem["lo_sum_ready"], 1)
            pe.wait_ge(sem["small_loaded"], 7 * 16)

            def transposes(pair, first):
                for u in range(2):
                    pe.wait_ge(sem["sub_normed"], 2 * SUB * pair + SUB * (u + 1))
                    if first:
                        pe.wait_ge(sem["flag_ready"], 1)
                    else:
                        pe.wait_ge(sem["q_first"], 2 * pair + u - 1)
                    for s in range(SUB):
                        last = nc.tensor.transpose(ps_prep[:, u, s * P:(s + 1) * P], xn_nat[:, u, s], mem["ident"][:])
                    last.then_inc(sem["transposed"], 1)

            def q_product(pair):
                for u in range(2):
                    pe.wait_ge(sem["xn_hi_done"], 2 * pair + u + 1)
                    pe.wait_ge(sem["xn_lo_done"], 2 * pair + u + 1)
                    terms = [(w, a) for w in (w_hi, w_lo) for a in (xn_hi, xn_lo)]
                    for n, (w, a) in enumerate(terms):
                        last = nc.tensor.matmul(ps_prep[:, u], w[:, WQ:WQ + P], a[:, u], start=(n == 0), stop=(n == len(terms) - 1))
                    last.then_inc(sem["q_product"], 1)

            def up(p, u, parts):
                for b in range(KB):
                    j = KB * u + b
                    slot_is_free(pe, p, j)
                    for half, at in ((0, W1), (1, W2)):
                        terms = [(w, a) for w in parts for a in (xn_hi, xn_lo)]
                        for n, (w, a) in enumerate(terms):
                            last = nc.tensor.matmul(ps_ff[:, j % FF_SLOTS, half], w[:, at + b * P:at + (b + 1) * P], a[:, u],
                                                    start=(n == 0), stop=(n == len(terms) - 1))
                    last.then_inc(sem["up_done"], 1)

            def hidden(p, layer, u, parts):
                at = (None, H1, H2)[layer]
                h_ready(pe, p, 8 * (layer - 1) + KB * (u + 1))
                for b in range(KB):
                    j = 8 + 4 * (layer - 1) + 2 * u + b // 2
                    if b % 2 == 0:
                        slot_is_free(pe, p, j)
                    terms = [(w, h, i) for i in range(KB) for w in parts for h in (h_hi, h_lo)]
                    for n, (w, h, i) in enumerate(terms):
                        c = at + i * HID + b * P
                        last = nc.tensor.matmul(ps_ff[:, j % FF_SLOTS, b % 2], w[:, c:c + P], h[:, (layer - 1) % 2, u, i],
                                                start=(n == 0), stop=(n == len(terms) - 1))
                    last.then_inc(sem["hidden_done"], 1)

            def down(p, u, parts):
                j = 16 + u
                slot_is_free(pe, p, j)
                h_ready(pe, p, 16 + KB * (u + 1))
                terms = [(w, h, i) for i in range(KB) for w in parts for h in (h_hi, h_lo)]
                for n, (w, h, i) in enumerate(terms):
                    c = W3 + i * P
                    last = nc.tensor.matmul(ps_ff[:, j % FF_SLOTS, 0], w[:, c:c + P], h[:, 0, u, i],
                                            start=(n == 0), stop=(n == len(terms) - 1))
                last.then_inc(sem["down_done"], 1)

            def pair_of_tiles(p, more, parts):
                up(p, 0, parts)
                up(p, 1, parts)
                hidden(p, 1, 0, parts)
                hidden(p, 1, 1, parts)
                if more:
                    transposes(p + 1, False)
                hidden(p, 2, 0, parts)
                if more:
                    q_product(p + 1)
                hidden(p, 2, 1, parts)
                down(p, 0, parts)
                down(p, 1, parts)

            def all_pairs(parts):
                with pe.Fori(0, PAIRS - 1) as p:
                    pair_of_tiles(p, True, parts)
                pair_of_tiles(PAIRS - 1, False, parts)

            transposes(0, True)
            q_product(0)
            general = pe.value_load(mem["flag"][0:1, 0:1])
            with pe.If(general != 0):
                all_pairs((w_hi, w_lo))
            with pe.Else():
                all_pairs((w_hi,))


FF_SEMS = ("sp_passed pool_passed dve_passed w_loaded w_hi_done w_split lo_max_ready lo_sum_ready flag_ready const_set small_loaded xT_first xT_second "
           "xT_loaded x_loaded0 x_loaded1 stats_done moments_done var_ready rstd_ready sub_normed transposed "
           "xn_hi_done xn_lo_done q_product q_first q_rest_ready q_second q_third q_stored0 q_stored1 up_done silu_done "
           "gated hidden_done gelu_full h_hi_done h_lo_done down_done ff_added").split()



MAX_FREE = EXP_FREE = PV_FREE = PROJ_FREE = Y_FREE = 2
SHIFT_DMAS = 16 * SHIFT_PARTS * CHUNKS
STAGE_DMAS = 16 * COLG


class Tile:

    def __init__(self, lap, at):
        self.lap, self.at = lap, at

    def __add__(self, n):
        return Tile(self.lap, self.at + n)

    def number(self):
        return self.lap * NBUF + self.at

    def laps(self, ring):
        return self.lap * (NBUF // ring) + self.at // ring

    def exists(self):
        return not isinstance(self.lap, int) or 0 <= self.number() < A_TILES

    def past(self, n):
        return not isinstance(self.lap, int) or self.number() >= n


def steps(engine, step):
    loops = (A_TILES - 5) // NBUF
    for t in range(-2, 2):
        step(Tile(0, t))
    with engine.Fori(0, loops) as lap:
        for at in range(2, 2 + NBUF):
            step(Tile(lap, at))
    for t in range(2 + NBUF * loops, A_TILES + 2):
        step(Tile(0, t))


def attention(nc, io, mem, sem):
    qk, qq, v_aug, probs = mem["qk"], mem["qq"], mem["v_aug"], mem["probs"]
    ps_max, ps_exp, ps_pv, ps_misc = mem["ps_max"], mem["ps_exp"], mem["ps_pv"], mem["ps_misc"]
    row_max, neg_max, shift_part = mem["row_max"], mem["neg_max"], mem["shift_part"]
    o_stage, o_feat, y_sum = mem["o_stage"], mem["o_feat"], mem["y_sum"]
    JC = NJ // CHUNKS

    with nc.Block() as block:
        @block.sync
        def _(sp):
            def q_rows(n, part, many):
                src = io["q_parts"][part:part + many].rearrange("c (d j) t -> (c d) j t", j=NJ)
                return src[:, :, bass.ds(n.number() * AT, AT)]

            def load_keys(n):
                if n.past(2):
                    wait_alone(sp, sem["keys_ready"], COLG * (n.number() - 1), sem["sp_passed"])
                for row, part, many in LOADS[0]:
                    sp.dma_start(mem["k_raw"][row * HD:(row + many) * HD, n.at % 2], q_rows(n, part, many)).then_inc(sem[f"k_loaded{n.at % 2}"], 16)

            def load_queries(n):
                if n.past(NBUF):
                    wait_alone(sp, sem["exp_mm"], NB * (n.number() - NBUF + 1), sem["sp_passed"])
                else:
                    wait_alone(sp, sem["zeros_set"], 2 * (n.number() + 1), sem["sp_passed"])
                for row, part, many in LOADS[1]:
                    sp.dma_start(qq[row * HD:(row + many) * HD, n.at % NBUF], q_rows(n, part, many)).then_inc(sem[f"q_loaded{n.at % NBUF}"], 16)

            def store_shift(n):
                cols = bass.ds(n.number() * AT, AT)
                wait_alone(sp, sem["shift_ready"], n.number() + 1, sem["sp_passed"])
                for c in range(CHUNKS):
                    for part in range(SHIFT_PARTS):
                        to = io["shift_rows"][part, c * JC:(c + 1) * JC, cols].rearrange("j (b t) -> b j t", t=HEAD_TOK)
                        sp.dma_start(to, shift_part[c * NB:(c + 1) * NB, n.at % 2, part].rearrange("b (j t) -> b j t", t=HEAD_TOK)
                                     ).then_inc(sem["shift_stored"], 16)

            def load_shift(n):
                cols = bass.ds(n.number() * AT, AT)
                wait_alone(sp, sem["shift_stored"], SHIFT_DMAS * (n.number() + 1), sem["sp_passed"])
                sp.dma_start(qq[SHIFT_AT:SHIFT_AT + SHIFT_PARTS, n.at % NBUF], io["shift_rows"][:, :, cols]).then_inc(sem[f"shift_set{n.at % 2}"], 16)

            def step(t):
                if (t + 3).exists():
                    load_keys(t + 3)
                if (t + 1).exists():
                    store_shift(t + 1)
                if (t + 3).exists():
                    load_queries(t + 3)
                if (t + 1).exists():
                    load_shift(t + 1)
                n = t + -2
                if n.exists():
                    wait_alone(sp, sem["y_done"], Y_FREE + n.number() + 1, sem["sp_passed"])
                    cols = bass.ds(n.number() * AT, AT)
                    sp.dma_start(io["out"][:, cols], y_sum[:, cols]).then_inc(sem["y_stored"], 16)

            load_keys(Tile(0, 0))
            load_queries(Tile(0, 0))
            sp.dma_start(mem["pick"][:], io["pick"]).then_inc(sem["b_small"], 16)
            sp.dma_start(mem["wu"][:], io["wu"]).then_inc(sem["b_small"], 16)
            sp.dma_start(mem["bias_u"][:], io["bu"]).then_inc(sem["b_small"], 16)
            steps(sp, step)
            wait_alone(sp, sem["y_stored"], 16 * A_TILES, sem["sp_passed"])

        @block.gpsimd
        def _(pool):
            def zeros_below(n):
                for i, rows in enumerate((slice(32, 64), slice(64, P))):
                    pool.memset(qq[rows, n].rearrange("p j t -> p (j t)"), 0.0).then_inc(sem["zeros_set"], 1)
                    wait_alone(pool, sem["zeros_set"], 2 * n + i + 1, sem["pool_passed"])

            zeros_below(0)
            pool.memset(v_aug[:].rearrange("p n c v -> p (n c v)"), 0.0).then_inc(sem["v_set"], 1)
            wait_alone(pool, sem["v_set"], 1, sem["pool_passed"])
            pool.memset(v_aug[:, :, :, HD:2 * HD], 1.0).then_inc(sem["v_set"], 1)
            wait_alone(pool, sem["v_set"], 2, sem["pool_passed"])
            for n in range(1, NBUF):
                zeros_below(n)

            def second_part(n):
                wait_alone(pool, sem["shift_first"], n.number() + 1, sem["pool_passed"])
                nc.gpsimd.tensor_tensor(shift_part[:, n.at % 2, 1], neg_max[:], shift_part[:, n.at % 2, 0], ALU.subtract).then_inc(sem["shift_ready"], 1)

            def to_features(n):
                b = n.at % 2
                wait_alone(pool, sem["pv_out"], PV_FREE + GROUPS * (n.number() + 1), sem["pool_passed"])
                for c in range(COLG):
                    to = io["o_rows"][:, :, bass.ds(n.number() * AT + c * GROUPS * HEAD_TOK, GROUPS * HEAD_TOK)]
                    src = o_stage[PV_ROWS * c:PV_ROWS * c + 2 * HD, b].rearrange("p j s t -> p j (s t)")
                    pool.dma_start(to, src).then_inc(sem[f"o_written{b}"], 16)
                wait_alone(pool, sem[f"o_written{b}"], STAGE_DMAS * (n.laps(2) + 1), sem["pool_passed"])
                wait_alone(pool, sem["projected"], PROJ_FREE + n.number() - 1, sem["pool_passed"])
                cols = bass.ds(n.number() * AT, AT)
                pool.dma_start(o_feat[:, b], io["o_rows"].rearrange("(w d) j t -> (d j) w t", w=2)[:, :, cols]).then_inc(sem[f"o_read{b}"], 16)

            def divide_by_sum(n):
                b = n.at % 2
                wait_alone(pool, sem["sum_inverted"], n.number() + 1, sem["pool_passed"])
                nc.gpsimd.tensor_tensor(o_feat[:, b, 0], o_feat[:, b, 0], o_feat[:, b, 1], ALU.mult).then_inc(sem["o_normed"], 1)

            def step(t):
                if (t + -2).exists():
                    divide_by_sum(t + -2)
                if (t + 1).exists():
                    second_part(t + 1)
                if (t + -1).exists():
                    to_features(t + -1)

            steps(pool, step)

        @block.vector
        def _(dve):
            dve.sem_inc(sem["max_done"], MAX_FREE)
            dve.sem_inc(sem["y_done"], Y_FREE)

            def ones_below(n):
                for rows in (slice(32, 64), slice(64, P)):
                    dve.memset(qk[rows, n].rearrange("p b c -> p (b c)"), 1.0).then_inc(sem["ones_set"], 1)

            ones_below(0)
            dve.wait_ge(sem["ones_set"], 2)

            def keys_in_order(n, part):
                if part == 0:
                    dve.wait_ge(sem[f"k_loaded{n.at % 2}"], KEYS_LOADED * (n.laps(2) + 1))
                    if n.past(4):
                        dve.wait_ge(sem["exp_mm"], NB * (n.number() - 3))
                bs = slice(part * NB // 4, (part + 1) * NB // 4)
                src = mem["k_raw"][:, n.at % 2].rearrange("p j (b t) -> p b j t", t=HEAD_TOK)[:, bs]
                nc.vector.tensor_copy(qk[0:ROWS, n.at % NBUF, bs].rearrange("p b (j t) -> p b j t", t=HEAD_TOK), src).then_inc(sem["keys_ready"], 1)

            for part in range(2):
                keys_in_order(Tile(0, 0), part)
            for n in range(1, NBUF):
                ones_below(n)
            dve.wait_ge(sem["ones_set"], 2 * NBUF)
            dve.wait_ge(sem["b_small"], 3 * 16)

            def step(t):
                n, old = t + 2, t + -2
                for k in range(NB):
                    if n.exists():
                        at = block_of(k)
                        dve.wait_ge(sem["max_mm"], NB * n.number() + k + 1)
                        nc.vector.tensor_reduce(out=row_max[:, n.at % 2, :, at], in_=ps_max[:, k % 2].rearrange("p (c q) -> p c q", q=POS),
                                                axis=AX.X, op=ALU.max).then_inc(sem["max_done"], 1)
                    if k in (9, 13) and (t + 3).exists():
                        keys_in_order(t + 3, (k - 9) // 4)
                    if old.exists() and k == 2:
                        b = old.at % 2
                        dve.wait_ge(sem[f"o_read{b}"], 16 * (old.laps(2) + 1))
                        nc.vector.reciprocal(o_feat[:, b, 1], o_feat[:, b, 1]).then_inc(sem["sum_inverted"], 1)
                    if old.exists() and k == 11:
                        dve.wait_ge(sem["projected"], PROJ_FREE + old.number() + 1)
                        to = y_sum[:, bass.ds(old.number() * AT, AT)]
                        nc.vector.scalar_tensor_tensor(out=to, in0=ps_misc[:, (t.at + 1) % 2, 0:AT], scalar=mem["bias_u"][:, 0:1], in1=to,
                                                       op0=ALU.add, op1=ALU.add).then_inc(sem["y_done"], 1)

            steps(dve, step)

        @block.scalar
        def _(act):
            act.sem_inc(sem["exp_done"], EXP_FREE)
            act.sem_inc(sem["pv_out"], PV_FREE)
            act.wait_ge(sem["v_set"], 2)
            act.wait_ge(sem["ones_set"], 2)

            def keys_in_order(n, part):
                if part == 2:
                    act.wait_ge(sem[f"k_loaded{n.at % 2}"], KEYS_LOADED * (n.laps(2) + 1))
                    if n.past(4):
                        act.wait_ge(sem["exp_mm"], NB * (n.number() - 3))
                bs = slice(part * NB // 4, (part + 1) * NB // 4)
                src = mem["k_raw"][:, n.at % 2].rearrange("p j (b t) -> p b j t", t=HEAD_TOK)[:, bs]
                nc.scalar.activation(qk[0:ROWS, n.at % NBUF, bs].rearrange("p b (j t) -> p b j t", t=HEAD_TOK), src, ACT.Copy).then_inc(sem["keys_ready"], 1)

            def values_out(n):
                act.wait_ge(sem["max_mm"], NB * (n.number() + 1))
                src = ps_misc[:, n.at % 2, 0:NB * CHUNKS * HD].rearrange("p (c v) -> p c v", v=HD)
                nc.scalar.activation(v_aug[:, n.at % NBUF, :, 0:HD], src, ACT.Copy).then_inc(sem["v_done"], 1)

            def shift_out(n):
                b = n.at % 2
                act.wait_ge(sem["max_turned"], n.number() + 1)
                if n.past(1):
                    act.wait_ge(sem["shift_ready"], n.number())
                if n.past(2):
                    act.wait_ge(sem["shift_stored"], SHIFT_DMAS * (n.number() - 1))
                src = ps_misc[0:CHUNKS * NB, (n.at + 0) % 2, 0:P]
                nc.scalar.activation(neg_max[:], src, ACT.Copy, scale=-1.0)
                nc.scalar.activation(shift_part[:, b, 0], src, ACT.Copy, scale=-1.0).then_inc(sem["shift_first"], 1)

            def pv_out(n, s):
                done = GROUPS * n.number() + s
                act.wait_ge(sem["pv_mm"], PV_FREE + done + 1)
                if s == 0 and n.past(2):
                    act.wait_ge(sem[f"o_written{n.at % 2}"], STAGE_DMAS * n.laps(2))
                nc.scalar.activation(o_stage[:, n.at % 2, :, s], ps_pv[:, s % 2, 0:POS].rearrange("p (j t) -> p j t", t=HEAD_TOK),
                                     ACT.Copy).then_inc(sem["pv_out"], 1)

            def step(t):
                for k in range(NB):
                    s = k // COLG
                    if t.exists():
                        act.wait_ge(sem["exp_mm"], NB * t.number() + k + 1)
                        if k % COLG == 0:
                            act.wait_ge(sem["pv_mm"], PV_FREE + GROUPS * t.number() + s - 1)
                        nc.scalar.activation(probs[:, k % (2 * COLG)], ps_exp[:, k % 2], ACT.Exp, scale=SCORE_SCALE).then_inc(sem["exp_done"], 1)
                    if k == 0 and (t + 1).exists():
                        values_out(t + 1)
                    if k == 2 and (t + 1).exists():
                        shift_out(t + 1)
                    if k in (9, 13) and (t + 3).exists():
                        keys_in_order(t + 3, 2 + (k - 9) // 4)
                    if k % COLG == COLG - 1:
                        n = t if s else t + -1
                        if n.exists():
                            pv_out(n, (s - 1) % GROUPS)

            for part in range(2, 4):
                keys_in_order(Tile(0, 0), part)
            act.wait_ge(sem["ones_set"], 2 * NBUF)
            steps(act, step)

        @block.tensor
        def _(pe):
            pe.sem_inc(sem["pv_mm"], PV_FREE)
            pe.sem_inc(sem["projected"], PROJ_FREE)
            pe.wait_ge(sem["b_small"], 3 * 16)

            def keys(n, k, c, rows):
                return qk[0:rows, n.at % NBUF, block_of(k), c * P:(c + 1) * P]

            def queries(n, k, rows):
                at = block_of(k) * HEAD_TOK
                return qq[0:rows, n.at % NBUF, :, at:at + HEAD_TOK]

            def scores(n, k, rows, bank, values=None):
                for c in range(CHUNKS):
                    if values is not None:
                        col = (CHUNKS * k + c) * HD
                        nc.tensor.matmul(values[:, col:col + HD], keys(n, k, c, SHIFT_AT), mem["pick"][:], start=True, stop=True)
                    last = nc.tensor.matmul(bank[:, c * POS:(c + 1) * POS], keys(n, k, c, rows), queries(n, k, rows), start=True, stop=True)
                return last

            def weighted_values(n, s, c):
                done = GROUPS * n.number() + s
                if c == 0:
                    pe.wait_ge(sem["exp_done"], EXP_FREE + COLG * (done + 1))
                    pe.wait_ge(sem["pv_out"], PV_FREE + done - 1)
                    if s == 0:
                        pe.wait_ge(sem["v_done"], n.number() + 1)
                for g in range(COLG):
                    k = COLG * s + g
                    last = nc.tensor.matmul(ps_pv[PV_ROWS * g:PV_ROWS * (g + 1), s % 2, 0:POS], v_aug[:, n.at % NBUF, CHUNKS * k + c],
                                            probs[:, k % (2 * COLG), c * POS:(c + 1) * POS], start=(c == 0), stop=(c == CHUNKS - 1))
                if c == CHUNKS - 1:
                    last.then_inc(sem["pv_mm"], 1)

            def step(t):
                n, old = t + 2, t + -2
                for k in range(NB):
                    s = k // COLG
                    if n.exists():
                        if k == 0:
                            if isinstance(n.lap, int) and n.number() < NBUF:
                                pe.wait_ge(sem["ones_set"], 2 * (n.number() + 1))
                            pe.wait_ge(sem["keys_ready"], COLG * (n.number() + 1))
                            pe.wait_ge(sem[f"q_loaded{n.at % NBUF}"], QUERIES_LOADED * (n.laps(NBUF) + 1))
                            if t.past(0):
                                pe.wait_ge(sem["shift_first"], t.number() + 1)
                            if t.past(3):
                                pe.wait_ge(sem["y_done"], Y_FREE + t.number() - 2)
                        pe.wait_ge(sem["max_done"], MAX_FREE + NB * n.number() + k - 1)
                        scores(n, k, SHIFT_AT, ps_max[:, k % 2], ps_misc[:, n.at % 2]).then_inc(sem["max_mm"], 1)
                    if k == 2 and (t + 1).exists():
                        pe.wait_ge(sem["max_done"], MAX_FREE + NB * (t.number() + 2))
                        pe.wait_ge(sem["v_done"], t.number() + 2)
                        nc.tensor.transpose(ps_misc[0:CHUNKS * NB, (t.at + 1) % 2, 0:P],
                                            row_max[:, (t.at + 1) % 2].rearrange("p c b -> p (c b)"), mem["ident"][:]).then_inc(sem["max_turned"], 1)
                    if t.exists():
                        if k == 0:
                            pe.wait_ge(sem[f"shift_set{t.at % 2}"], 16 * (t.laps(2) + 1))
                        pe.wait_ge(sem["exp_done"], EXP_FREE + NB * t.number() + k - 1)
                        scores(t, k, P, ps_exp[:, k % 2]).then_inc(sem["exp_mm"], 1)
                    if k == 9 and old.exists():
                        pe.wait_ge(sem["o_normed"], old.number() + 1)
                        if (t + 1).exists():
                            pe.wait_ge(sem["shift_first"], t.number() + 2)
                        pe.wait_ge(sem["y_done"], Y_FREE + old.number() - 1)
                        nc.tensor.matmul(ps_misc[:, (t.at + 1) % 2, 0:AT], mem["wu"][:], o_feat[:, old.at % 2, 0], start=True, stop=True
                                         ).then_inc(sem["projected"], 1)
                    if k % 2 == 1:
                        m = t if s else t + -1
                        if m.exists():
                            weighted_values(m, (s - 1) % GROUPS, (k % COLG) // 2)

            steps(pe, step)


B_SEMS = ("b_small ones_set zeros_set v_set k_loaded0 k_loaded1 keys_ready q_loaded0 q_loaded1 q_loaded2 q_loaded3 max_mm max_done max_turned shift_first shift_ready "
          "shift_stored shift_set0 shift_set1 exp_mm exp_done pv_mm pv_out v_done o_written0 o_written1 o_read0 o_read1 "
          "sum_inverted o_normed projected y_done y_stored").split()

INPUTS = ("x xT w1 w2 h1 h2 w3 wq wu w1s w2s h1s h2s w3s bq bu ident pick").split()


def build(nc, arrays):
    io = {n: nc.dram_tensor(f"in_{n}", arrays[f"in_{n}"].shape, mybir.dt.from_np(arrays[f"in_{n}"].dtype), kind="ExternalInput").ap()
          for n in INPUTS}
    io["out"] = nc.dram_tensor("out_T", (EMB, TOKENS), F32, kind="ExternalOutput").ap()
    io["q_parts"] = nc.dram_tensor("q_parts", (3, EMB, TOKENS), BF16, kind="Internal").ap()
    io["o_rows"] = nc.dram_tensor("o_rows", (2 * HD, NJ, TOKENS), F32, kind="Internal").ap()
    io["shift_rows"] = nc.dram_tensor("shift_rows", (SHIFT_PARTS, NJ, TOKENS), BF16, kind="Internal").ap()
    with ExitStack() as both:
        def sbuf(stack, name, shape, dtype=F32):
            mem[name] = stack.enter_context(nc.sbuf_tensor(name, shape, dtype))

        def psum(stack, name, shape):
            mem[name] = stack.enter_context(nc.psum_tensor(name, shape, F32))

        mem = {}
        sbuf(both, "y_sum", [P, TOKENS])
        sbuf(both, "ident", [P, P])
        sem = {n: both.enter_context(nc.semaphore(n)) for n in FF_SEMS + B_SEMS}
        with ExitStack() as a:
            for name, shape, dtype in (
                    ("w_hi", [P, WCOLS], F32R), ("w_lo", [P, WCOLS], F32R), ("h_hi", [P, 2, 2, KB, TT], F32R), ("h_lo", [P, 2, 2, KB, TT], F32R),
                    ("hf", [P, HF_RING, TT], F32), ("silu_out", [P, 2, TT], F32), ("x_nat", [P, 2, SUB, P], F32), ("xn_nat", [P, 2, SUB, P], F32),
                    ("xn_hi", [P, 2, TT], F32R), ("xn_lo", [P, 2, TT], F32R), ("q_full", [P, 2, TT], F32), ("q_rest", [P, 2, TT], F32),
                    ("q_part", [P, 2, 3, TT], BF16), ("stats", [P, 2 * SUB, 6], F32), ("moments", [P, 2 * SUB, 2], F32),
                    ("var_eps", [P, 2 * SUB], F32), ("rstd", [P, 2 * SUB], F32), ("minus_half", [P, 2 * SUB], F32),
                    ("scales", [P, 4 * KB + 1], F32), ("bias_q", [P, 1], F32), ("ones", [P, 1], F32), ("lo_max", [P, 1], F32), ("flag", [1, 1], I32)):
                sbuf(a, name, shape, dtype)
            psum(a, "ps_ff", [P, FF_SLOTS, 2, TT])
            psum(a, "ps_prep", [P, 2, TT])
            feed_forward(nc, io, mem, sem)
        with ExitStack() as b:
            for name, shape, dtype in (
                    ("qk", [P, NBUF, NB, POS], BF16), ("k_raw", [ROWS, 2, NJ, AT], BF16), ("qq", [P, NBUF, NJ, AT], BF16), ("v_aug", [P, NBUF, NB * CHUNKS, PV_ROWS], F32),
                    ("probs", [P, 2 * COLG, CHUNKS * POS], F32), ("row_max", [P, 2, CHUNKS, NB], F32), ("neg_max", [CHUNKS * NB, P], F32),
                    ("shift_part", [CHUNKS * NB, 2, SHIFT_PARTS, P], BF16), ("o_stage", [P, 2, NJ, GROUPS, HEAD_TOK], F32),
                    ("o_feat", [P, 2, 2, AT], F32), ("wu", [P, P], F32), ("bias_u", [P, 1], F32), ("pick", [SHIFT_AT, HD], BF16)):
                sbuf(b, name, shape, dtype)
            psum(b, "ps_max", [P, 2, 512])
            psum(b, "ps_exp", [P, 2, 512])
            psum(b, "ps_pv", [P, 2, 512])
            psum(b, "ps_misc", [P, 2, 512])
            attention(nc, io, mem, sem)


def kernel(L0_attn_x, L0_attn_wq, L0_attn_bq, L0_attn_wu, L0_attn_bu, L0_ffn_w1_w, L0_ffn_w1_s, L0_ffn_w2_w, L0_ffn_w2_s,
           L0_ffn_h1_w, L0_ffn_h1_s, L0_ffn_h2_w, L0_ffn_h2_s, L0_ffn_w3_w, L0_ffn_w3_s):
    import concourse.bacc as bacc
    import ml_dtypes
    from concourse.bass_utils import run_bass_kernel_spmd

    def laid(a):
        return np.ascontiguousarray(np.asarray(a))

    x = laid(L0_attn_x).reshape(TOKENS, EMB)
    order = np.arange(EMB).reshape(NJ, HD).T.ravel()
    pick = np.zeros((SHIFT_AT, HD), ml_dtypes.bfloat16)
    for block, part in enumerate(PARTS_OF_KEYS):
        if part not in PARTS_OF_KEYS[:block]:
            pick[block * HD + np.arange(HD), np.arange(HD)] = 1
    columns = lambda s: laid(np.asarray(s).reshape(-1, P).T)
    arrays = {
        "in_x": x, "in_xT": laid(x.T),
        "in_w1": laid(np.asarray(L0_ffn_w1_w).T), "in_w2": laid(np.asarray(L0_ffn_w2_w).T),
        "in_h1": laid(np.asarray(L0_ffn_h1_w).T), "in_h2": laid(np.asarray(L0_ffn_h2_w).T), "in_w3": laid(np.asarray(L0_ffn_w3_w).T),
        "in_wq": laid(np.asarray(L0_attn_wq)[order].T), "in_wu": laid(np.asarray(L0_attn_wu).T[order]),
        "in_w1s": columns(L0_ffn_w1_s), "in_w2s": columns(L0_ffn_w2_s), "in_h1s": columns(L0_ffn_h1_s), "in_h2s": columns(L0_ffn_h2_s),
        "in_w3s": columns(L0_ffn_w3_s), "in_bq": columns(np.asarray(L0_attn_bq)[order]), "in_bu": columns(L0_attn_bu),
        "in_ident": np.eye(P, dtype=np.float32), "in_pick": pick,
    }
    nc = bacc.Bacc("TRN2", target_bir_lowering=False, num_devices=1)
    build(nc, arrays)
    result = run_bass_kernel_spmd(nc, [arrays], core_ids=[0])
    return laid(result.results[0]["out_T"].T).reshape(BATCH, SEQ, EMB)
```

```python
from contextlib import ExitStack

import numpy as np
import concourse.bass as bass
from concourse import mybir
from concourse.alu_op_type import AluOpType as ALU

F32 = mybir.dt.float32
F32R = mybir.dt.float32r
BF16 = mybir.dt.bfloat16
I32 = mybir.dt.int32
ACT = mybir.ActivationFunctionType
AX = mybir.AxisListType

BATCH, SEQ, EMB, HID = 32, 256, 128, 512
TOKENS = BATCH * SEQ
P = 128
HEADS = 16
HD = EMB // HEADS
NJ = EMB // HD
HEAD_TOK = SEQ // NJ
POS = SEQ
EPS = 1e-5
SCORE_SCALE = 1.0 / float(np.sqrt(EMB))

TT = 512
SUB = TT // P
KB = HID // P
PAIRS = TOKENS // (2 * TT)
HF_RING = 4
COPY_LAG, LAG = 2, 3
OPS = 3 * 2 * KB
FF_SLOTS = 3

WQ, W1, W2 = 0, P, P + HID
H1, H2 = W2 + HID, W2 + HID + KB * HID
W3 = H2 + KB * HID
WCOLS = W3 + KB * P
SECTIONS = (WQ, H1), (H1, H2), (H2, WCOLS)
SCALES, BIAS_Q, BIAS_U, IDENT, WU = 0, 4 * KB + 1, 4 * KB + 2, 4 * KB + 3, 4 * KB + 3 + P
SMALL = WU + P

AT = 256
NB = AT // HEAD_TOK
A_TILES = TOKENS // AT
COLG = 4
GROUPS = NB // COLG
INVERT_AT, KEYS_AT, PROJECT_AT, ADD_AT = (2, 6), (4, 9, 11), 12, 13
KEY_PARTS, DVE_PARTS = 4, len(KEYS_AT)
NBUF = 4
CHUNKS = POS // P
PARTS_OF_KEYS, PARTS_OF_QUERIES = (0, 1, 2, 0, 1, 2, 0, 1), (0, 1, 0, 1, 2, 1, 2, 0)
ROWS = len(PARTS_OF_KEYS) * HD
SHIFT_AT = 96
SHIFT_PARTS = 2
PV_ROWS = 32


def runs(parts):
    found = []
    for place, part in enumerate(parts):
        if found and part == found[-1][1] + found[-1][2]:
            found[-1][2] += 1
        else:
            found.append([place, part, 1])
    return found


KEY_LOADS, QUERY_LOADS = runs(PARTS_OF_KEYS), runs(PARTS_OF_QUERIES)
KEYS_LOADED, QUERIES_LOADED = 16 * len(KEY_LOADS), 16 * len(QUERY_LOADS)


def block_of(k):
    return COLG * (k % COLG) + k // COLG


def wait_alone(engine, semaphore, value, passed):
    engine.wait_ge(semaphore, value)
    engine.sem_inc(passed, 1)


class Tile:

    def __init__(self, lap, at):
        self.lap, self.at = lap, at

    def __add__(self, n):
        return Tile(self.lap, self.at + n)

    def number(self):
        return self.lap * NBUF + self.at

    def laps(self, ring):
        return self.lap * (NBUF // ring) + self.at // ring

    def exists(self):
        return not isinstance(self.lap, int) or 0 <= self.number() < A_TILES

    def past(self, n):
        return not isinstance(self.lap, int) or self.number() >= n


def q_rows(io, n, part, many):
    src = io["q_parts"][part:part + many].rearrange("c (d j) t -> (c d) j t", j=NJ)
    return src[:, :, bass.ds(n.number() * AT, AT)]


def feed_forward(nc, io, mem, sem):
    ps_ff, ps_prep = mem["ps_ff"], mem["ps_prep"]
    w_hi, w_lo, h_hi, h_lo = mem["w_hi"], mem["w_lo"], mem["h_hi"], mem["h_lo"]
    hf, silu_out, y_sum = mem["hf"], mem["silu_out"], mem["y_sum"]
    x_nat, xn_nat, xn_hi, xn_lo = mem["x_nat"], mem["xn_nat"], mem["xn_hi"], mem["xn_lo"]
    q_full, q_rest, q_part = mem["q_full"], mem["q_rest"], mem["q_part"]
    stats, moments, var_eps, rstd = mem["stats"], mem["moments"], mem["var_eps"], mem["rstd"]
    scales, bias_q = mem["scales"], mem["bias_q"]
    FREE = 2

    def slot_is_free(pe, p, j):
        before, pair = (j - FF_SLOTS, p) if j >= FF_SLOTS else (j - FF_SLOTS + 18, p - 1)
        if before < 8:
            pe.wait_ge(sem["gated"], FREE + 8 * pair + before + 1)
        elif before < 16:
            pe.wait_ge(sem["gelu_full"], 16 + 16 * pair + 2 * (before - 8) + 2)
        else:
            pe.wait_ge(sem["ff_added"], FREE + 2 * pair + before - 16 + 1)

    def by_pool(k):
        return k < 2 * KB and k % 2 == 1

    def low_made(wait, p, k):
        pool_made = sum(by_pool(i) for i in range(k))
        wait(sem["h_lo_done"], HF_RING + (OPS - KB) * p + k - pool_made)
        if pool_made:
            wait(sem["h_lo_pool"], KB * p + pool_made)

    def h_ready(pe, p, k):
        pe.wait_ge(sem["h_hi_done"], HF_RING + OPS * p + k)
        low_made(pe.wait_ge, p, k)

    with nc.Block() as block:
        @block.sync
        def _(sp):
            def load_x(u, pair, first):
                if not first:
                    wait_alone(sp, sem["sub_normed"], 2 * SUB * pair, sem["sp_passed"])
                src = io["x"].rearrange("(n s p) e -> p n s e", p=P, s=SUB)
                if first:
                    src = src[:, u]
                else:
                    src = src[:, bass.ds(2 * pair + u, 1)].rearrange("p o s e -> p (o s) e")
                sp.dma_start(x_nat[:, u], src).then_inc(sem[f"x_loaded{u}"], 16)

            for u in range(2):
                load_x(u, 0, True)
            staged = y_sum[:, TOKENS - WCOLS:]
            for n, (first, end) in enumerate(SECTIONS):
                sp.dma_start(staged[:, first:end], io["weights"][:, first:end]).then_inc(sem[f"w_loaded{n}"], 16)
            wait_alone(sp, sem["w_split"], len(SECTIONS), sem["sp_passed"])
            sp.dma_start(y_sum[:], io["xT"]).then_inc(sem["xT_loaded"], 16)

            def store_q(u, pair):
                wait_alone(sp, sem["q_third"], 2 * pair + u + 1, sem["sp_passed"])
                to = io["q_parts"][:, :, bass.ds((2 * pair + u) * TT, TT)].rearrange("c f t -> f c t")
                sp.dma_start(to, q_part[:, u]).then_inc(sem[f"q_stored{u}"], 16)

            for u in range(2):
                store_q(u, 0)
            with sp.Fori(0, PAIRS - 1) as p:
                for u in range(2):
                    load_x(u, p + 1, False)
                for u in range(2):
                    store_q(u, p + 1)
            for u in range(2):
                wait_alone(sp, sem[f"q_stored{u}"], 16 + 16 * PAIRS, sem["sp_passed"])
            sp.dma_start(mem["pick"][:], io["pick"]).then_inc(sem["pick_loaded"], 16)
            for n in (Tile(0, 0), Tile(0, 1)):
                for row, part, many in KEY_LOADS:
                    sp.dma_start(mem["k_raw"][row * HD:(row + many) * HD, n.at], q_rows(io, n, part, many)).then_inc(sem[f"k_loaded{n.at}"], 16)

        @block.gpsimd
        def _(pool):
            pool.dma_start(mem["small"][:], io["small"]).then_inc(sem["small_loaded"], 16)
            pool.memset(mem["minus_half"][:], -0.5).then_inc(sem["const_set"], 1)
            wait_alone(pool, sem["const_set"], 1, sem["pool_passed"])

            def inverse_deviation(pair):
                wait_alone(pool, sem["var_ready"], pair + 1, sem["pool_passed"])
                nc.gpsimd.tensor_tensor(rstd[:], var_eps[:], mem["minus_half"][:], ALU.pow).then_inc(sem["rstd_ready"], 1)

            def q_remainders(pair):
                for u in range(2):
                    wait_alone(pool, sem["q_first"], 2 * pair + u + 1, sem["pool_passed"])
                    nc.gpsimd.tensor_tensor(q_rest[:, u], q_full[:, u], q_part[:, u, 0], ALU.subtract).then_inc(sem["q_rest_ready"], 1)
                for u in range(2):
                    wait_alone(pool, sem["q_second"], 2 * pair + u + 1, sem["pool_passed"])
                    nc.gpsimd.tensor_tensor(q_part[:, u, 2], q_rest[:, u], q_part[:, u, 1], ALU.subtract).then_inc(sem["q_third"], 1)

            def low_parts(p):
                for k in range(2 * KB):
                    if by_pool(k):
                        wait_alone(pool, sem["gated"], FREE + 8 * p + k + 1, sem["pool_passed"])
                        wait_alone(pool, sem["h_hi_done"], HF_RING + OPS * p + k + 1, sem["pool_passed"])
                        nc.gpsimd.tensor_tensor(h_lo[:, 0, k // KB, k % KB], hf[:, k % HF_RING], h_hi[:, 0, k // KB, k % KB].bitcast(F32),
                                                ALU.subtract).then_inc(sem["h_lo_pool"], 1)

            inverse_deviation(0)
            q_remainders(0)
            with pool.Fori(0, PAIRS - 1) as p:
                low_parts(p)
                inverse_deviation(p + 1)
                q_remainders(p + 1)
            low_parts(PAIRS - 1)

        @block.vector
        def _(dve):
            dve.sem_inc(sem["gated"], FREE)
            dve.sem_inc(sem["ff_added"], FREE)
            dve.sem_inc(sem["h_lo_done"], HF_RING)
            dve.memset(mem["ones"][:], 1.0).then_inc(sem["ones_ready"], 1)

            def split_weights(n):
                first, end = SECTIONS[n]
                dve.wait_ge(sem["w_hi_done"], n + 1)
                nc.vector.tensor_tensor(w_lo[:, first:end], y_sum[:, TOKENS - WCOLS + first:TOKENS - WCOLS + end],
                                        w_hi[:, first:end].bitcast(F32), ALU.subtract).then_inc(sem["w_split"], 1)

            def largest_low(n):
                first, end = SECTIONS[n]
                dve.wait_ge(sem["w_split"], n + 1)
                nc.vector.tensor_reduce(out=mem["lo_max"][:, n:n + 1], in_=w_lo[:, max(first, W1):end].bitcast(F32), axis=AX.X, op=ALU.max,
                                        apply_absolute_value=True).then_inc(sem["lo_max_ready"], 1)

            def norm_inputs(pair):
                for u in range(2):
                    dve.wait_ge(sem[f"x_loaded{u}"], 16 * (pair + 1))
                    for s in range(SUB):
                        nc.vector.bn_stats(out=stats[:, u * SUB + s], in_=x_nat[:, u, s]).then_inc(sem["stats_done"], 1)
                for n in range(2 * SUB):
                    if n == 0:
                        wait_alone(dve, sem["stats_done"], 2 * SUB * (pair + 1), sem["dve_passed"])
                    nc.vector.bn_aggr(out=moments[:, n], in_=stats[:, n]).then_inc(sem["moments_done"], 1)
                dve.wait_ge(sem["moments_done"], 2 * SUB * (pair + 1))
                nc.vector.tensor_scalar(var_eps[:], moments[:, :, 1], EPS, None, ALU.add).then_inc(sem["var_ready"], 1)
                dve.wait_ge(sem["rstd_ready"], pair + 1)
                dve.wait_ge(sem["transposed"], 2 + 2 * pair)
                for n in range(2 * SUB):
                    u, s = n // SUB, n % SUB
                    nc.vector.tensor_scalar(xn_nat[:, u, s], x_nat[:, u, s], moments[:, n, 0:1], rstd[:, n:n + 1],
                                            ALU.subtract, ALU.mult).then_inc(sem["sub_normed"], 1)

            def lo_part(p, k, layer, u, b):
                if layer == 0:
                    dve.wait_ge(sem["gated"], FREE + 8 * p + k + 1)
                else:
                    dve.wait_ge(sem["gelu_full"], 16 + 16 * p + (k - 8) + 1)
                dve.wait_ge(sem["h_hi_done"], HF_RING + OPS * p + k + 1)
                nc.vector.tensor_tensor(h_lo[:, layer % 2, u, b], hf[:, k % HF_RING], h_hi[:, layer % 2, u, b].bitcast(F32),
                                        ALU.subtract).then_inc(sem["h_lo_done"], 1)

            def xn_low(pair):
                for u in range(2):
                    dve.wait_ge(sem["xn_hi_done"], 2 * pair + u + 1)
                    nc.vector.tensor_tensor(xn_lo[:, u], ps_prep[:, u], xn_hi[:, u].bitcast(F32), ALU.subtract).then_inc(sem["xn_lo_done"], 1)

            def pair_of_tiles(p, more):
                for u in range(2):
                    for b in range(KB):
                        k, slot = KB * u + b, (KB * u + b) % FF_SLOTS
                        dve.wait_ge(sem["silu_done"], FREE + 8 * p + k + 1)
                        dve.wait_ge(sem["h_hi_done"], OPS * p + k + 1)
                        low_made(dve.wait_ge, p, k + 1 - HF_RING)
                        nc.vector.scalar_tensor_tensor(out=hf[:, k % HF_RING], in0=ps_ff[:, slot, 1], scalar=scales[:, KB + b:KB + b + 1],
                                                       in1=silu_out[:, k % 2], op0=ALU.mult, op1=ALU.mult).then_inc(sem["gated"], 1)
                        if k >= LAG and not by_pool(k - LAG):
                            lo_part(p, k - LAG, 0, (k - LAG) // KB, (k - LAG) % KB)
                for k in range(2 * KB - LAG, 2 * KB):
                    if not by_pool(k):
                        lo_part(p, k, 0, k // KB, k % KB)
                if more:
                    norm_inputs(p + 1)
                for u in range(2):
                    for b in range(KB):
                        lo_part(p, 8 + KB * u + b, 1, u, b)
                if more:
                    xn_low(p + 1)
                for u in range(2):
                    for b in range(KB):
                        lo_part(p, 16 + KB * u + b, 2, u, b)
                if more:
                    q_seconds(p + 1)
                for u in range(2):
                    slot = (16 + u) % FF_SLOTS
                    dve.wait_ge(sem["down_done"], 2 * p + u + 1)
                    dve.wait_ge(sem["xT_loaded"], 16)
                    to = y_sum[:, bass.ds((2 * p + u) * TT, TT)]
                    nc.vector.scalar_tensor_tensor(out=to, in0=ps_ff[:, slot, 0], scalar=scales[:, 4 * KB:4 * KB + 1], in1=to,
                                                   op0=ALU.mult, op1=ALU.add).then_inc(sem["ff_added"], 1)

            def q_seconds(pair):
                for u in range(2):
                    dve.wait_ge(sem["q_rest_ready"], 2 * pair + u + 1)
                    nc.vector.tensor_copy(q_part[:, u, 1], q_rest[:, u]).then_inc(sem["q_second"], 1)

            norm_inputs(0)
            split_weights(0)
            xn_low(0)
            split_weights(1)
            largest_low(0)
            largest_low(1)
            split_weights(2)
            largest_low(2)
            dve.wait_ge(sem["lo_sum_ready"], 1)
            nc.vector.tensor_reduce(out=mem["lo_any"][:], in_=ps_ff[0:1, 0, 0, 0:len(SECTIONS)], axis=AX.X, op=ALU.max).then_inc(sem["flag_ready"], 1)
            dve.wait_ge(sem["flag_ready"], 1)
            nc.vector.tensor_scalar(mem["flag"][:], mem["lo_any"][:], 0.0, None, ALU.not_equal).then_inc(sem["flag_ready"], 1)
            q_seconds(0)
            dve.wait_ge(sem["small_loaded"], 16)
            with dve.Fori(0, PAIRS - 1) as p:
                pair_of_tiles(p, True)
            pair_of_tiles(PAIRS - 1, False)

        @block.scalar
        def _(act):
            act.sem_inc(sem["gelu_full"], 16)
            act.sem_inc(sem["h_hi_done"], HF_RING)
            act.sem_inc(sem["silu_done"], FREE)
            for u in range(2):
                act.sem_inc(sem[f"q_stored{u}"], 16)

            def high_weights(n):
                first, end = SECTIONS[n]
                act.wait_ge(sem[f"w_loaded{n}"], 16)
                nc.scalar.activation(w_hi[:, first:end], y_sum[:, TOKENS - WCOLS + first:TOKENS - WCOLS + end], ACT.Identity).then_inc(sem["w_hi_done"], 1)

            def xn_high(pair):
                for u in range(2):
                    act.wait_ge(sem["transposed"], 2 + 2 * pair + u + 1)
                    nc.scalar.activation(xn_hi[:, u], ps_prep[:, u], ACT.Identity).then_inc(sem["xn_hi_done"], 1)

            def q_out(pair):
                for u in range(2):
                    act.wait_ge(sem["q_product"], 2 * pair + u + 1)
                    act.wait_ge(sem[f"q_stored{u}"], 16 + 16 * pair)
                    nc.scalar.activation(q_full[:, u], ps_prep[:, u], ACT.Identity, bias=bias_q[:, 0:1])
                    nc.scalar.activation(q_part[:, u, 0], ps_prep[:, u], ACT.Identity, bias=bias_q[:, 0:1]).then_inc(sem["q_first"], 1)

            def silu(p, k):
                act.wait_ge(sem["up_done"], 8 * p + k + 1)
                act.wait_ge(sem["gated"], 8 * p + k + 1)
                nc.scalar.activation(silu_out[:, k % 2], ps_ff[:, k % FF_SLOTS, 0], ACT.Silu, scale=scales[:, k % KB:k % KB + 1]).then_inc(sem["silu_done"], 1)

            def high_copy(p, k):
                act.wait_ge(sem["gated"], FREE + 8 * p + k + 1)
                nc.scalar.activation(h_hi[:, 0, k // KB, k % KB], hf[:, k % HF_RING], ACT.Identity).then_inc(sem["h_hi_done"], 1)

            def gelu(p, layer, u, b):
                k = 8 * layer + KB * u + b
                slot = 8 + (k - 8) // 2
                src = ps_ff[:, slot % FF_SLOTS, b % 2]
                s = scales[:, (1 + layer) * KB + b:(1 + layer) * KB + b + 1]
                act.wait_ge(sem["hidden_done"], 16 * p + (k - 8) + 1)
                nc.scalar.activation(h_hi[:, layer % 2, u, b], src, ACT.Gelu, scale=s).then_inc(sem["h_hi_done"], 1)
                low_made(act.wait_ge, p, k + 1 - HF_RING)
                act.wait_ge(sem["h_hi_done"], OPS * p + k + 1)
                nc.scalar.activation(hf[:, k % HF_RING], src, ACT.Gelu, scale=s).then_inc(sem["gelu_full"], 1)

            def pair_of_tiles(p, more):
                for k in range(2 * KB + COPY_LAG):
                    if k < 2 * KB:
                        silu(p, k)
                    if k >= COPY_LAG:
                        high_copy(p, k - COPY_LAG)
                for u in range(2):
                    for b in range(KB):
                        gelu(p, 1, u, b)
                if more:
                    xn_high(p + 1)
                for u in range(2):
                    for b in range(KB):
                        gelu(p, 2, u, b)
                    if more and u == 0:
                        q_out(p + 1)

            high_weights(0)
            high_weights(1)
            xn_high(0)
            high_weights(2)
            act.wait_ge(sem["small_loaded"], 16)
            q_out(0)
            with act.Fori(0, PAIRS - 1) as p:
                pair_of_tiles(p, True)
            pair_of_tiles(PAIRS - 1, False)

        @block.tensor
        def _(pe):
            pe.sem_inc(sem["transposed"], 2)
            pe.wait_ge(sem["small_loaded"], 16)

            def transposes(pair, first):
                for u in range(2):
                    pe.wait_ge(sem["sub_normed"], 2 * SUB * pair + SUB * (u + 1))
                    if not first:
                        pe.wait_ge(sem["q_first"], 2 * pair + u - 1)
                    for s in range(SUB):
                        last = nc.tensor.transpose(ps_prep[:, u, s * P:(s + 1) * P], xn_nat[:, u, s], mem["ident"][:])
                    last.then_inc(sem["transposed"], 1)

            def q_product(pair):
                for u in range(2):
                    pe.wait_ge(sem["xn_hi_done"], 2 * pair + u + 1)
                    pe.wait_ge(sem["xn_lo_done"], 2 * pair + u + 1)
                    terms = [(w, a) for w in (w_hi, w_lo) for a in (xn_hi, xn_lo)]
                    for n, (w, a) in enumerate(terms):
                        last = nc.tensor.matmul(ps_prep[:, u], w[:, WQ:WQ + P], a[:, u], start=(n == 0), stop=(n == len(terms) - 1))
                    last.then_inc(sem["q_product"], 1)

            def up(p, u, parts):
                for b in range(KB):
                    j = KB * u + b
                    slot_is_free(pe, p, j)
                    for half, at in ((0, W1), (1, W2)):
                        terms = [(w, a) for w in parts for a in (xn_hi, xn_lo)]
                        for n, (w, a) in enumerate(terms):
                            last = nc.tensor.matmul(ps_ff[:, j % FF_SLOTS, half], w[:, at + b * P:at + (b + 1) * P], a[:, u],
                                                    start=(n == 0), stop=(n == len(terms) - 1))
                    last.then_inc(sem["up_done"], 1)

            def hidden(p, layer, u, parts):
                at = (None, H1, H2)[layer]
                for b in range(KB):
                    j = 8 + 4 * (layer - 1) + 2 * u + b // 2
                    if b % 2 == 0:
                        slot_is_free(pe, p, j)
                    terms = [(w, h, i) for i in range(KB) for w in parts for h in (h_hi, h_lo)]
                    for n, (w, h, i) in enumerate(terms):
                        if b == 0 and (n == 0 or i != terms[n - 1][2]):
                            h_ready(pe, p, 8 * (layer - 1) + KB * u + i + 1)
                        c = at + i * HID + b * P
                        last = nc.tensor.matmul(ps_ff[:, j % FF_SLOTS, b % 2], w[:, c:c + P], h[:, (layer - 1) % 2, u, i],
                                                start=(n == 0), stop=(n == len(terms) - 1))
                    last.then_inc(sem["hidden_done"], 1)

            def down(p, u, parts):
                j = 16 + u
                slot_is_free(pe, p, j)
                terms = [(w, h, i) for i in range(KB) for w in parts for h in (h_hi, h_lo)]
                for n, (w, h, i) in enumerate(terms):
                    if n == 0 or i != terms[n - 1][2]:
                        h_ready(pe, p, 16 + KB * u + i + 1)
                    c = W3 + i * P
                    last = nc.tensor.matmul(ps_ff[:, j % FF_SLOTS, 0], w[:, c:c + P], h[:, 0, u, i],
                                            start=(n == 0), stop=(n == len(terms) - 1))
                last.then_inc(sem["down_done"], 1)

            def pair_of_tiles(p, more, parts):
                up(p, 0, parts)
                up(p, 1, parts)
                hidden(p, 1, 0, parts)
                hidden(p, 1, 1, parts)
                if more:
                    transposes(p + 1, False)
                hidden(p, 2, 0, parts)
                if more:
                    q_product(p + 1)
                hidden(p, 2, 1, parts)
                down(p, 0, parts)
                down(p, 1, parts)

            def all_pairs(parts):
                with pe.Fori(0, PAIRS - 1) as p:
                    pair_of_tiles(p, True, parts)
                pair_of_tiles(PAIRS - 1, False, parts)

            transposes(0, True)
            pe.wait_ge(sem["w_hi_done"], 1)
            pe.wait_ge(sem["w_split"], 1)
            q_product(0)
            pe.wait_ge(sem["lo_max_ready"], len(SECTIONS))
            pe.wait_ge(sem["ones_ready"], 1)
            nc.tensor.matmul(ps_ff[0:1, 0, 0, 0:len(SECTIONS)], mem["ones"][:], mem["lo_max"][:], start=True, stop=True).then_inc(sem["lo_sum_ready"], 1)
            pe.wait_ge(sem["w_split"], len(SECTIONS))
            pe.wait_ge(sem["flag_ready"], 2)
            general = pe.value_load(mem["flag"][0:1, 0:1])
            with pe.If(general != 0):
                all_pairs((w_hi, w_lo))
            with pe.Else():
                all_pairs((w_hi,))


FF_SEMS = ("sp_passed pool_passed dve_passed w_loaded0 w_loaded1 w_loaded2 w_hi_done w_split lo_max_ready lo_sum_ready flag_ready const_set ones_ready small_loaded "
           "xT_loaded x_loaded0 x_loaded1 stats_done moments_done var_ready rstd_ready sub_normed transposed "
           "xn_hi_done xn_lo_done q_product q_first q_rest_ready q_second q_third q_stored0 q_stored1 up_done silu_done "
           "gated hidden_done gelu_full h_hi_done h_lo_done h_lo_pool down_done ff_added").split()



POOL_FILLS = (1, 3, 5, 7)
MAX_FREE = 4
EXP_FREE = PV_FREE = PROJ_FREE = Y_FREE = 2
SHIFT_DMAS = 16 * SHIFT_PARTS * CHUNKS


def steps(engine, step):
    loops = (A_TILES - 5) // NBUF
    for t in range(-2, 2):
        step(Tile(0, t))
    with engine.Fori(0, loops) as lap:
        for at in range(2, 2 + NBUF):
            step(Tile(lap, at))
    for t in range(2 + NBUF * loops, A_TILES + 2):
        step(Tile(0, t))


def max_bank(k):
    return k % 3 if k < NB - 1 else 1


def max_bank_before(k):
    return max(i for i in range(-NB, k) if max_bank(i % NB) == max_bank(k))


def back(t, group):
    return (t, group) if group >= 0 else (t + -1, group + GROUPS)


def attention(nc, io, mem, sem):
    qk, qq, v_aug, probs = mem["qk"], mem["qq"], mem["v_aug"], mem["probs"]
    ps_max, ps_exp, ps_pv, ps_misc = mem["ps_max"], mem["ps_exp"], mem["ps_pv"], mem["ps_misc"]
    row_max, neg_max, shift_part = mem["row_max"], mem["neg_max"], mem["shift_part"]
    o_stage, o_feat, y_sum = mem["o_stage"], mem["o_feat"], mem["y_sum"]
    JC = NJ // CHUNKS

    with nc.Block() as block:
        @block.sync
        def _(sp):
            def load_keys(n):
                if n.past(2):
                    wait_alone(sp, sem["keys_by_dve"], DVE_PARTS * (n.number() - 1), sem["sp_passed"])
                    wait_alone(sp, sem["keys_by_act"], (KEY_PARTS - DVE_PARTS) * (n.number() - 1), sem["sp_passed"])
                for row, part, many in KEY_LOADS:
                    sp.dma_start(mem["k_raw"][row * HD:(row + many) * HD, n.at % 2], q_rows(io, n, part, many)).then_inc(sem[f"k_loaded{n.at % 2}"], 16)

            def load_queries(n):
                if n.past(NBUF):
                    wait_alone(sp, sem["exp_mm"], NB * (n.number() - NBUF + 1), sem["sp_passed"])
                for row, part, many in QUERY_LOADS:
                    sp.dma_start(qq[row * HD:(row + many) * HD, n.at % NBUF], q_rows(io, n, part, many)).then_inc(sem[f"q_loaded{n.at % NBUF}"], 16)

            def store_shift(n):
                cols = bass.ds(n.number() * AT, AT)
                wait_alone(sp, sem["shift_ready"], n.number() + 1, sem["sp_passed"])
                for c in range(CHUNKS):
                    for part in range(SHIFT_PARTS):
                        to = io["shift_rows"][part, c * JC:(c + 1) * JC, cols].rearrange("j (b t) -> b j t", t=HEAD_TOK)
                        sp.dma_start(to, shift_part[c * NB:(c + 1) * NB, n.at % 2, part].rearrange("b (j t) -> b j t", t=HEAD_TOK)
                                     ).then_inc(sem["shift_stored"], 16)

            def load_shift(n):
                cols = bass.ds(n.number() * AT, AT)
                wait_alone(sp, sem["shift_stored"], SHIFT_DMAS * (n.number() + 1), sem["sp_passed"])
                sp.dma_start(qq[SHIFT_AT:SHIFT_AT + SHIFT_PARTS, n.at % NBUF], io["shift_rows"][:, :, cols]).then_inc(sem[f"shift_set{n.at % 2}"], 16)

            def read_features(n):
                b, groups = n.at % 2, io["o_rows"][bass.ds(n.number() * COLG, COLG)]
                wait_alone(sp, sem[f"o_written{b}"], 16 * (n.laps(2) + 1), sem["sp_passed"])
                wait_alone(sp, sem["projected"], PROJ_FREE + n.number() - 1, sem["sp_passed"])
                for w in range(2):
                    rows = groups[:, w * HD:(w + 1) * HD].rearrange("g d (j c) -> (d j) g c", j=NJ)
                    sp.dma_start(o_feat[:, b, w].rearrange("p (g c) -> p g c", g=COLG), rows).then_inc(sem[f"o_read{b}"], 16)

            def step(t):
                if (t + 3).exists() and (t + 3).past(2):
                    load_keys(t + 3)
                if (t + 1).exists():
                    store_shift(t + 1)
                if (t + 3).exists():
                    load_queries(t + 3)
                if (t + 1).exists():
                    load_shift(t + 1)
                if (t + -1).exists():
                    read_features(t + -1)
                n = t + -2
                if n.exists():
                    wait_alone(sp, sem["y_done"], Y_FREE + n.number() + 1, sem["sp_passed"])
                    cols = bass.ds(n.number() * AT, AT)
                    sp.dma_start(io["out"][:, cols], y_sum[:, cols]).then_inc(sem["y_stored"], 16)

            load_queries(Tile(0, 0))
            steps(sp, step)
            wait_alone(sp, sem["y_stored"], 16 * A_TILES, sem["sp_passed"])

        @block.gpsimd
        def _(pool):
            def fill_operands(n):
                if n > 0:
                    pool.memset(qk[ROWS:P, n].rearrange("p b c -> p (b c)"), 1.0).then_inc(sem["rows_set"], 1)
                    wait_alone(pool, sem["rows_set"], POOL_FILLS[n] - 1, sem["pool_passed"])
                pool.memset(qq[ROWS:P, n].rearrange("p j t -> p (j t)"), 0.0).then_inc(sem["rows_set"], 1)
                wait_alone(pool, sem["rows_set"], POOL_FILLS[n], sem["pool_passed"])

            fill_operands(0)
            fill_operands(1)
            pool.memset(v_aug[:].rearrange("p n c v -> p (n c v)"), 0.0).then_inc(sem["v_set"], 1)
            wait_alone(pool, sem["v_set"], 1, sem["pool_passed"])
            pool.memset(v_aug[:, :, :, HD:2 * HD], 1.0).then_inc(sem["v_set"], 1)
            wait_alone(pool, sem["v_set"], 2, sem["pool_passed"])

            def second_part(n):
                wait_alone(pool, sem["shift_first"], n.number() + 1, sem["pool_passed"])
                nc.gpsimd.tensor_tensor(shift_part[:, n.at % 2, 1], neg_max[:], shift_part[:, n.at % 2, 0], ALU.subtract).then_inc(sem["shift_ready"], 1)

            def write_rows(n):
                b = n.at % 2
                wait_alone(pool, sem["pv_out"], PV_FREE + GROUPS * (n.number() + 1), sem["pool_passed"])
                to = io["o_rows"][bass.ds(n.number() * COLG, COLG)].rearrange("g r c -> (g r) c")
                pool.dma_start(to, o_stage[:, b].rearrange("p j s t -> p (j s t)")).then_inc(sem[f"o_written{b}"], 16)

            def divide_by_sum(n):
                b = n.at % 2
                wait_alone(pool, sem["sum_inverted"], len(INVERT_AT) * (n.number() + 1), sem["pool_passed"])
                nc.gpsimd.tensor_tensor(o_feat[:, b, 0], o_feat[:, b, 0], o_feat[:, b, 1], ALU.mult).then_inc(sem["o_normed"], 1)

            def step(t):
                if (t + 1).exists():
                    second_part(t + 1)
                if (t + 3).past(2) and not (t + 3).past(NBUF):
                    fill_operands((t + 3).number())
                if (t + -1).exists():
                    write_rows(t + -1)
                if (t + -2).exists():
                    divide_by_sum(t + -2)

            steps(pool, step)

        @block.vector
        def _(dve):
            dve.sem_inc(sem["max_done"], MAX_FREE)
            dve.sem_inc(sem["y_done"], Y_FREE)

            def keys_in_order(n, part):
                if part == 0:
                    dve.wait_ge(sem[f"k_loaded{n.at % 2}"], KEYS_LOADED * (n.laps(2) + 1))
                    if n.past(4):
                        dve.wait_ge(sem["exp_mm"], NB * (n.number() - 3))
                bs = slice(part * NB // KEY_PARTS, (part + 1) * NB // KEY_PARTS)
                src = mem["k_raw"][:, n.at % 2].rearrange("p j (b t) -> p b j t", t=HEAD_TOK)[:, bs]
                nc.vector.tensor_copy(qk[0:ROWS, n.at % NBUF, bs].rearrange("p b (j t) -> p b j t", t=HEAD_TOK), src).then_inc(sem["keys_by_dve"], 1)

            for part in range(DVE_PARTS):
                keys_in_order(Tile(0, 0), part)
            dve.memset(qk[ROWS:P, 0].rearrange("p b c -> p (b c)"), 1.0).then_inc(sem["ones_set"], 1)

            def step(t):
                n, old = t + 2, t + -2
                for k in range(NB):
                    if n.exists():
                        at = block_of(k)
                        dve.wait_ge(sem["max_mm"], NB * n.number() + k + 1)
                        nc.vector.tensor_reduce(out=row_max[:, n.at % 2, :, at], in_=ps_max[:, max_bank(k)].rearrange("p (c q) -> p c q", q=POS),
                                                axis=AX.X, op=ALU.max).then_inc(sem["max_done"], 1)
                    if k in KEYS_AT and (t + 3).exists():
                        keys_in_order(t + 3, KEYS_AT.index(k))
                    if old.exists() and k in INVERT_AT:
                        b, part = old.at % 2, AT // len(INVERT_AT)
                        cols = slice(INVERT_AT.index(k) * part, (INVERT_AT.index(k) + 1) * part)
                        if k == INVERT_AT[0]:
                            dve.wait_ge(sem[f"o_read{b}"], 2 * 16 * (old.laps(2) + 1))
                        nc.vector.reciprocal(o_feat[:, b, 1, cols], o_feat[:, b, 1, cols]).then_inc(sem["sum_inverted"], 1)
                    if old.exists() and k == ADD_AT:
                        dve.wait_ge(sem["projected"], PROJ_FREE + old.number() + 1)
                        to = y_sum[:, bass.ds(old.number() * AT, AT)]
                        nc.vector.scalar_tensor_tensor(out=to, in0=ps_misc[:, (t.at + 1) % 2, 0:AT], scalar=mem["bias_u"][:, 0:1], in1=to,
                                                       op0=ALU.add, op1=ALU.add).then_inc(sem["y_done"], 1)

            steps(dve, step)

        @block.scalar
        def _(act):
            act.sem_inc(sem["exp_done"], EXP_FREE)
            act.sem_inc(sem["pv_out"], PV_FREE)

            def keys_in_order(n, part):
                if part == DVE_PARTS:
                    act.wait_ge(sem[f"k_loaded{n.at % 2}"], KEYS_LOADED * (n.laps(2) + 1))
                    if n.past(4):
                        act.wait_ge(sem["exp_mm"], NB * (n.number() - 3))
                bs = slice(part * NB // KEY_PARTS, (part + 1) * NB // KEY_PARTS)
                src = mem["k_raw"][:, n.at % 2].rearrange("p j (b t) -> p b j t", t=HEAD_TOK)[:, bs]
                nc.scalar.activation(qk[0:ROWS, n.at % NBUF, bs].rearrange("p b (j t) -> p b j t", t=HEAD_TOK), src, ACT.Copy).then_inc(sem["keys_by_act"], 1)

            def values_out(n):
                if not n.past(NBUF):
                    act.wait_ge(sem["v_set"], 2)
                act.wait_ge(sem["max_mm"], NB * (n.number() + 1))
                src = ps_misc[:, n.at % 2, 0:NB * CHUNKS * HD].rearrange("p (c v) -> p c v", v=HD)
                nc.scalar.activation(v_aug[:, n.at % NBUF, :, 0:HD], src, ACT.Copy).then_inc(sem["v_done"], 1)

            def shift_out(n):
                b = n.at % 2
                act.wait_ge(sem["max_turned"], n.number() + 1)
                if n.past(1):
                    act.wait_ge(sem["shift_ready"], n.number())
                if n.past(2):
                    act.wait_ge(sem["shift_stored"], SHIFT_DMAS * (n.number() - 1))
                src = ps_misc[0:CHUNKS * NB, n.at % 2, 0:P]
                nc.scalar.activation(neg_max[:], src, ACT.Copy, scale=-1.0)
                nc.scalar.activation(shift_part[:, b, 0], src, ACT.Copy, scale=-1.0).then_inc(sem["shift_first"], 1)

            def pv_out(n, s):
                done = GROUPS * n.number() + s
                act.wait_ge(sem["pv_mm"], PV_FREE + done + 1)
                if s == 0 and n.past(2):
                    act.wait_ge(sem[f"o_written{n.at % 2}"], 16 * n.laps(2))
                nc.scalar.activation(o_stage[:, n.at % 2, :, s], ps_pv[:, 0:POS].rearrange("p (j t) -> p j t", t=HEAD_TOK),
                                     ACT.Copy).then_inc(sem["pv_out"], 1)

            def step(t):
                for k in range(NB):
                    s = k // COLG
                    m, group = back(t, s - 2)
                    if k % COLG == 0 and m.exists():
                        pv_out(m, group)
                    if t.exists():
                        act.wait_ge(sem["exp_mm"], NB * t.number() + k + 1)
                        if k % COLG == 0:
                            act.wait_ge(sem["pv_mm"], PV_FREE + GROUPS * t.number() + s - 1)
                        nc.scalar.activation(probs[:, k % (2 * COLG)], ps_exp[:, k % 2], ACT.Exp, scale=SCORE_SCALE).then_inc(sem["exp_done"], 1)
                    if k == 0 and (t + 1).exists():
                        values_out(t + 1)
                    if k == 2 and (t + 1).exists():
                        shift_out(t + 1)
                    if k == 9 and (t + 3).exists():
                        keys_in_order(t + 3, DVE_PARTS)

            keys_in_order(Tile(0, 0), DVE_PARTS)
            steps(act, step)

        @block.tensor
        def _(pe):
            pe.sem_inc(sem["pv_mm"], PV_FREE)
            pe.sem_inc(sem["projected"], PROJ_FREE)
            pe.wait_ge(sem["pick_loaded"], 16)

            def keys(n, k, c, rows):
                return qk[0:rows, n.at % NBUF, block_of(k), c * P:(c + 1) * P]

            def queries(n, k, rows):
                at = block_of(k) * HEAD_TOK
                return qq[0:rows, n.at % NBUF, :, at:at + HEAD_TOK]

            def scores(n, k, rows, bank, values=None):
                for c in range(CHUNKS):
                    if values is not None:
                        col = (CHUNKS * k + c) * HD
                        nc.tensor.matmul(values[:, col:col + HD], keys(n, k, c, SHIFT_AT), mem["pick"][:], start=True, stop=True)
                    last = nc.tensor.matmul(bank[:, c * POS:(c + 1) * POS], keys(n, k, c, rows), queries(n, k, rows), start=True, stop=True)
                return last

            def weighted_values(n, s, c):
                done = GROUPS * n.number() + s
                if c == 0:
                    pe.wait_ge(sem["exp_done"], EXP_FREE + COLG * (done + 1))
                    pe.wait_ge(sem["pv_out"], PV_FREE + done)
                    if s == 0:
                        pe.wait_ge(sem["v_done"], n.number() + 1)
                for g in range(COLG):
                    k = COLG * s + g
                    last = nc.tensor.matmul(ps_pv[PV_ROWS * g:PV_ROWS * (g + 1), 0:POS], v_aug[:, n.at % NBUF, CHUNKS * k + c],
                                            probs[:, k % (2 * COLG), c * POS:(c + 1) * POS], start=(c == 0), stop=(c == CHUNKS - 1))
                if c == CHUNKS - 1:
                    last.then_inc(sem["pv_mm"], 1)

            def maxima(t, k):
                n = t + 2
                if k == 0:
                    if not n.past(NBUF):
                        pe.wait_ge(sem["ones_set"], 1)
                        pe.wait_ge(sem["rows_set"], POOL_FILLS[n.number()])
                    pe.wait_ge(sem["keys_by_dve"], DVE_PARTS * (n.number() + 1))
                    pe.wait_ge(sem["keys_by_act"], (KEY_PARTS - DVE_PARTS) * (n.number() + 1))
                    pe.wait_ge(sem[f"q_loaded{n.at % NBUF}"], QUERIES_LOADED * (n.laps(NBUF) + 1))
                    if t.past(0):
                        pe.wait_ge(sem["shift_first"], t.number() + 1)
                    if t.past(3):
                        pe.wait_ge(sem["y_done"], Y_FREE + t.number() - 2)
                pe.wait_ge(sem["max_done"], MAX_FREE + NB * n.number() + max_bank_before(k) + 1)
                scores(n, k, SHIFT_AT, ps_max[:, max_bank(k)], ps_misc[:, n.at % 2]).then_inc(sem["max_mm"], 1)

            def exponents(t, k):
                if k == 0:
                    pe.wait_ge(sem[f"shift_set{t.at % 2}"], 16 * (t.laps(2) + 1))
                pe.wait_ge(sem["exp_done"], EXP_FREE + NB * t.number() + k - 1)
                scores(t, k, P, ps_exp[:, k % 2]).then_inc(sem["exp_mm"], 1)

            def turn_maxima(n):
                pe.wait_ge(sem["max_done"], MAX_FREE + NB * (n.number() + 1))
                pe.wait_ge(sem["v_done"], n.number() + 1)
                nc.tensor.transpose(ps_misc[0:CHUNKS * NB, n.at % 2, 0:P], row_max[:, n.at % 2].rearrange("p c b -> p (c b)"),
                                    mem["ident"][:]).then_inc(sem["max_turned"], 1)

            def project(t):
                old = t + -2
                pe.wait_ge(sem["o_normed"], old.number() + 1)
                if (t + 1).exists():
                    pe.wait_ge(sem["shift_first"], t.number() + 2)
                pe.wait_ge(sem["y_done"], Y_FREE + old.number() - 1)
                nc.tensor.matmul(ps_misc[:, (t.at + 1) % 2, 0:AT], mem["wu"][:], o_feat[:, old.at % 2, 0], start=True, stop=True
                                 ).then_inc(sem["projected"], 1)

            def step(t):
                for k in range(0, NB, 2):
                    if (t + 2).exists():
                        maxima(t, k)
                    s, c = k // COLG, 1 - k % COLG // 2
                    m, group = back(t, s - 1 - c)
                    if m.exists():
                        weighted_values(m, group, c)
                    if (t + 2).exists():
                        maxima(t, k + 1)
                    if t.exists():
                        exponents(t, k)
                    if k == 2 and (t + 1).exists():
                        turn_maxima(t + 1)
                    if k == PROJECT_AT and (t + -2).exists():
                        project(t)
                    if t.exists():
                        exponents(t, k + 1)

            steps(pe, step)


B_SEMS = ("pick_loaded ones_set rows_set v_set k_loaded0 k_loaded1 keys_by_dve keys_by_act q_loaded0 q_loaded1 q_loaded2 q_loaded3 max_mm max_done max_turned shift_first shift_ready "
          "shift_stored shift_set0 shift_set1 exp_mm exp_done pv_mm pv_out v_done o_written0 o_written1 o_read0 o_read1 "
          "sum_inverted o_normed projected y_done y_stored").split()

INPUTS = ("x", "xT", "weights", "small", "pick")


def build(nc, arrays):
    io = {n: nc.dram_tensor(f"in_{n}", arrays[f"in_{n}"].shape, mybir.dt.from_np(arrays[f"in_{n}"].dtype), kind="ExternalInput").ap()
          for n in INPUTS}
    io["out"] = nc.dram_tensor("out_T", (EMB, TOKENS), F32, kind="ExternalOutput").ap()
    io["q_parts"] = nc.dram_tensor("q_parts", (3, EMB, TOKENS), BF16, kind="Internal").ap()
    io["o_rows"] = nc.dram_tensor("o_rows", (A_TILES * COLG, PV_ROWS, NJ * GROUPS * HEAD_TOK), F32, kind="Internal").ap()
    io["shift_rows"] = nc.dram_tensor("shift_rows", (SHIFT_PARTS, NJ, TOKENS), BF16, kind="Internal").ap()
    with ExitStack() as both:
        def sbuf(stack, name, shape, dtype=F32):
            mem[name] = stack.enter_context(nc.sbuf_tensor(name, shape, dtype))

        def psum(stack, name, shape):
            mem[name] = stack.enter_context(nc.psum_tensor(name, shape, F32))

        mem = {}
        sbuf(both, "y_sum", [P, TOKENS])
        for name, shape, dtype in (("small", [P, SMALL], F32), ("k_raw", [ROWS, 2, NJ, AT], BF16), ("pick", [SHIFT_AT, HD], BF16)):
            sbuf(both, name, shape, dtype)
        for name, first, end in (("scales", SCALES, BIAS_Q), ("bias_q", BIAS_Q, BIAS_U), ("bias_u", BIAS_U, IDENT), ("ident", IDENT, WU), ("wu", WU, SMALL)):
            mem[name] = mem["small"][:, first:end]
        sem = {n: both.enter_context(nc.semaphore(n)) for n in FF_SEMS + B_SEMS}
        with ExitStack() as a:
            for name, shape, dtype in (
                    ("w_hi", [P, WCOLS], F32R), ("w_lo", [P, WCOLS], F32R), ("h_hi", [P, 2, 2, KB, TT], F32R), ("h_lo", [P, 2, 2, KB, TT], F32R),
                    ("hf", [P, HF_RING, TT], F32), ("silu_out", [P, 2, TT], F32), ("x_nat", [P, 2, SUB, P], F32), ("xn_nat", [P, 2, SUB, P], F32),
                    ("xn_hi", [P, 2, TT], F32R), ("xn_lo", [P, 2, TT], F32R), ("q_full", [P, 2, TT], F32), ("q_rest", [P, 2, TT], F32),
                    ("q_part", [P, 2, 3, TT], BF16), ("stats", [P, 2 * SUB, 6], F32), ("moments", [P, 2 * SUB, 2], F32),
                    ("var_eps", [P, 2 * SUB], F32), ("rstd", [P, 2 * SUB], F32), ("minus_half", [P, 2 * SUB], F32),
                    ("ones", [P, 1], F32), ("lo_max", [P, len(SECTIONS)], F32), ("lo_any", [1, 1], F32), ("flag", [1, 1], I32)):
                sbuf(a, name, shape, dtype)
            psum(a, "ps_ff", [P, FF_SLOTS, 2, TT])
            psum(a, "ps_prep", [P, 2, TT])
            feed_forward(nc, io, mem, sem)
        with ExitStack() as b:
            for name, shape, dtype in (
                    ("qk", [P, NBUF, NB, POS], BF16), ("qq", [P, NBUF, NJ, AT], BF16), ("v_aug", [P, NBUF, NB * CHUNKS, PV_ROWS], F32),
                    ("probs", [P, 2 * COLG, CHUNKS * POS], F32), ("row_max", [P, 2, CHUNKS, NB], F32), ("neg_max", [CHUNKS * NB, P], F32),
                    ("shift_part", [CHUNKS * NB, 2, SHIFT_PARTS, P], BF16), ("o_stage", [P, 2, NJ, GROUPS, HEAD_TOK], F32),
                    ("o_feat", [P, 2, 2, AT], F32)):
                sbuf(b, name, shape, dtype)
            psum(b, "ps_max", [P, 3, 512])
            psum(b, "ps_exp", [P, 2, 512])
            psum(b, "ps_pv", [P, 512])
            psum(b, "ps_misc", [P, 2, 512])
            attention(nc, io, mem, sem)


def kernel(L0_attn_x, L0_attn_wq, L0_attn_bq, L0_attn_wu, L0_attn_bu, L0_ffn_w1_w, L0_ffn_w1_s, L0_ffn_w2_w, L0_ffn_w2_s,
           L0_ffn_h1_w, L0_ffn_h1_s, L0_ffn_h2_w, L0_ffn_h2_s, L0_ffn_w3_w, L0_ffn_w3_s):
    import concourse.bacc as bacc
    import ml_dtypes
    from concourse.bass_utils import run_bass_kernel_spmd

    def laid(a):
        return np.ascontiguousarray(np.asarray(a))

    x = laid(L0_attn_x).reshape(TOKENS, EMB)
    order = np.arange(EMB).reshape(NJ, HD).T.ravel()
    pick = np.zeros((SHIFT_AT, HD), ml_dtypes.bfloat16)
    for block, part in enumerate(PARTS_OF_KEYS):
        if part not in PARTS_OF_KEYS[:block]:
            pick[block * HD + np.arange(HD), np.arange(HD)] = 1

    def inputs_down(w):
        return np.asarray(w).T.reshape(-1, P, w.shape[0]).transpose(1, 0, 2).reshape(P, -1)

    def columns(v):
        return np.asarray(v).reshape(-1, P).T

    weights = [inputs_down(w) for w in (np.asarray(L0_attn_wq)[order], L0_ffn_w1_w, L0_ffn_w2_w, L0_ffn_h1_w, L0_ffn_h2_w, L0_ffn_w3_w)]
    small = [columns(v) for v in (L0_ffn_w1_s, L0_ffn_w2_s, L0_ffn_h1_s, L0_ffn_h2_s, L0_ffn_w3_s, np.asarray(L0_attn_bq)[order], L0_attn_bu)]
    small += [np.eye(P, dtype=np.float32), np.asarray(L0_attn_wu).T[order]]
    arrays = {"in_x": x, "in_xT": laid(x.T), "in_weights": laid(np.concatenate(weights, axis=1)), "in_small": laid(np.concatenate(small, axis=1)),
              "in_pick": pick}
    nc = bacc.Bacc("TRN2", target_bir_lowering=False, num_devices=1)
    build(nc, arrays)
    result = run_bass_kernel_spmd(nc, [arrays], core_ids=[0])
    return laid(result.results[0]["out_T"].T).reshape(BATCH, SEQ, EMB)
```
